# Optimizing a Trainium2 kernel written in Bass

```python
import numpy as np
import jax
import jax.numpy as jnp

def _softmax(x, axis=-1):
    return jax.nn.softmax(x, axis=axis)

def _gelu(x):
    return jax.nn.gelu(x, approximate=True)

def _silu(x):
    return jax.nn.silu(x)

def _sigmoid(x):
    return jax.nn.sigmoid(x)

def _layernorm(x, axis=-1, eps=1e-05):
    m = jnp.mean(x, axis=axis, keepdims=True)
    v = jnp.var(x, axis=axis, keepdims=True)
    return (x - m) / jnp.sqrt(v + eps)

def _scatter_add(tgt, idx, src, axis=0):
    return tgt.at[idx].add(src)

def _segment_sum(src, seg, n):
    return jax.ops.segment_sum(src, seg, n)
kernel_name = 'mk_seq_postln_d1_jaxref_r4_105703'

def setup_inputs(seed: int=0):
    np.random.seed(seed)
    _w = jnp.asarray

    def _L0_attn_setup():
        import jax, jax.numpy as jnp
        import numpy as np
        NUM_HEADS = 16
        LEVELS = 4

        def _mha(x, w_in, b_in, w_out, b_out):
            B, S, E = x.shape
            H = NUM_HEADS
            hd = E // H
            qkv = x @ w_in.T + b_in
            q, k, v = jnp.split(qkv, 3, axis=-1)
            split = lambda t: t.reshape(B, S, H, hd).transpose(0, 2, 1, 3)
            q, k, v = (split(q), split(k), split(v))
            scores = jnp.einsum('bhqd,bhkd->bhqk', q, k) / jnp.sqrt(jnp.asarray(hd, x.dtype))
            attn = jax.nn.softmax(scores, axis=-1)
            out = jnp.einsum('bhqk,bhkd->bhqd', attn, v)
            out = out.transpose(0, 2, 1, 3).reshape(B, S, E)
            return out @ w_out.T + b_out

        def _upsample_linear(x, target):
            B, L, E = x.shape
            src = (jnp.arange(target, dtype=jnp.float32) + 0.5) * (L / target) - 0.5
            src = jnp.clip(src, 0.0, L - 1)
            i0 = jnp.floor(src).astype(jnp.int32)
            i1 = jnp.minimum(i0 + 1, L - 1)
            w = (src - i0.astype(jnp.float32))[None, :, None].astype(x.dtype)
            return x[:, i0, :] * (1 - w) + x[:, i1, :] * w
        key = jax.random.key(seed)
        ks = jax.random.split(key, 7)
        B, S, E = (1, 512, 256)
        return {'query': jax.random.normal(ks[0], (B, S, E), jnp.float32), 'in_proj_w': jax.random.normal(ks[1], (LEVELS, 3 * E, E), jnp.float32) * 0.02, 'in_proj_b': jnp.zeros((LEVELS, 3 * E), jnp.float32), 'out_w': jax.random.normal(ks[2], (LEVELS, E, E), jnp.float32) * 0.02, 'out_b': jnp.zeros((LEVELS, E), jnp.float32), 'up_w': jax.random.normal(ks[3], (LEVELS - 1, E, E), jnp.float32) * 0.02, 'up_b': jnp.zeros((LEVELS - 1, E), jnp.float32)}
    _L0_attn_in = _L0_attn_setup()

    def _L0_ffn_setup():
        import jax, jax.numpy as jnp
        import numpy as np
        D_IN, D_HID = (256, 1024)

        def _ternary(key, shape):
            return jax.random.randint(key, shape, -1, 2).astype(jnp.float32)

        def _tlin(x, w, s):
            return jnp.einsum('bsi,oi->bso', x, w) * s
        key = jax.random.key(seed)
        ks = jax.random.split(key, 12)
        inv = lambda fan: 1.0 / np.sqrt(fan).astype(np.float32)
        return {'x': jax.random.normal(ks[0], (4, 512, D_IN), dtype=jnp.float32), 'w1_w': _ternary(ks[1], (D_HID, D_IN)), 'w1_s': jax.random.uniform(ks[2], (D_HID,), dtype=jnp.float32) * inv(D_IN), 'w2_w': _ternary(ks[3], (D_HID, D_IN)), 'w2_s': jax.random.uniform(ks[4], (D_HID,), dtype=jnp.float32) * inv(D_IN), 'h1_w': _ternary(ks[5], (D_HID, D_HID)), 'h1_s': jax.random.uniform(ks[6], (D_HID,), dtype=jnp.float32) * inv(D_HID), 'h2_w': _ternary(ks[7], (D_HID, D_HID)), 'h2_s': jax.random.uniform(ks[8], (D_HID,), dtype=jnp.float32) * inv(D_HID), 'w3_w': _ternary(ks[9], (D_IN, D_HID)), 'w3_s': jax.random.uniform(ks[10], (D_IN,), dtype=jnp.float32) * inv(D_HID)}
    _L0_ffn_in = _L0_ffn_setup()
    _d = {'L0_attn_query': _L0_attn_in['query'], 'L0_attn_in_proj_w': _L0_attn_in['in_proj_w'], 'L0_attn_in_proj_b': _L0_attn_in['in_proj_b'], 'L0_attn_out_w': _L0_attn_in['out_w'], 'L0_attn_out_b': _L0_attn_in['out_b'], 'L0_attn_up_w': _L0_attn_in['up_w'], 'L0_attn_up_b': _L0_attn_in['up_b'], 'L0_ffn_w1_w': _L0_ffn_in['w1_w'], 'L0_ffn_w1_s': _L0_ffn_in['w1_s'], 'L0_ffn_w2_w': _L0_ffn_in['w2_w'], 'L0_ffn_w2_s': _L0_ffn_in['w2_s'], 'L0_ffn_h1_w': _L0_ffn_in['h1_w'], 'L0_ffn_h1_s': _L0_ffn_in['h1_s'], 'L0_ffn_h2_w': _L0_ffn_in['h2_w'], 'L0_ffn_h2_s': _L0_ffn_in['h2_s'], 'L0_ffn_w3_w': _L0_ffn_in['w3_w'], 'L0_ffn_w3_s': _L0_ffn_in['w3_s']}
    _x0 = _d['L0_attn_query']
    _d['L0_attn_query'] = jax.random.normal(jax.random.fold_in(jax.random.key(seed), 1), (8, 1024, 256), dtype=_x0.dtype)
    del _x0
    return _d

def reference(L0_attn_query, L0_attn_in_proj_w, L0_attn_in_proj_b, L0_attn_out_w, L0_attn_out_b, L0_attn_up_w, L0_attn_up_b, L0_ffn_w1_w, L0_ffn_w1_s, L0_ffn_w2_w, L0_ffn_w2_s, L0_ffn_h1_w, L0_ffn_h1_s, L0_ffn_h2_w, L0_ffn_h2_s, L0_ffn_w3_w, L0_ffn_w3_s):

    def _L0_attn_ref(query, in_proj_w, in_proj_b, out_w, out_b, up_w, up_b):
        import jax, jax.numpy as jnp
        import numpy as np
        NUM_HEADS = 16
        LEVELS = 4

        def _mha(x, w_in, b_in, w_out, b_out):
            B, S, E = x.shape
            H = NUM_HEADS
            hd = E // H
            qkv = x @ w_in.T + b_in
            q, k, v = jnp.split(qkv, 3, axis=-1)
            split = lambda t: t.reshape(B, S, H, hd).transpose(0, 2, 1, 3)
            q, k, v = (split(q), split(k), split(v))
            scores = jnp.einsum('bhqd,bhkd->bhqk', q, k) / jnp.sqrt(jnp.asarray(hd, x.dtype))
            attn = jax.nn.softmax(scores, axis=-1)
            out = jnp.einsum('bhqk,bhkd->bhqd', attn, v)
            out = out.transpose(0, 2, 1, 3).reshape(B, S, E)
            return out @ w_out.T + b_out

        def _upsample_linear(x, target):
            B, L, E = x.shape
            src = (jnp.arange(target, dtype=jnp.float32) + 0.5) * (L / target) - 0.5
            src = jnp.clip(src, 0.0, L - 1)
            i0 = jnp.floor(src).astype(jnp.int32)
            i1 = jnp.minimum(i0 + 1, L - 1)
            w = (src - i0.astype(jnp.float32))[None, :, None].astype(x.dtype)
            return x[:, i0, :] * (1 - w) + x[:, i1, :] * w
        B, S, E = query.shape
        outs = []
        for lvl in range(LEVELS):
            stride = 2 ** lvl
            x = query[:, ::stride, :]
            outs.append(_mha(x, in_proj_w[lvl], in_proj_b[lvl], out_w[lvl], out_b[lvl]))
        current = outs[-1]
        for lvl in range(LEVELS - 2, -1, -1):
            fine = outs[lvl]
            if current.shape[1] != fine.shape[1]:
                current = _upsample_linear(current, fine.shape[1])
            current = current @ up_w[lvl].T + up_b[lvl]
            current = current + fine
        return current

    def _L0_ffn_ref(x, w1_w, w1_s, w2_w, w2_s, h1_w, h1_s, h2_w, h2_s, w3_w, w3_s):
        import jax, jax.numpy as jnp
        import numpy as np
        D_IN, D_HID = (256, 1024)

        def _ternary(key, shape):
            return jax.random.randint(key, shape, -1, 2).astype(jnp.float32)

        def _tlin(x, w, s):
            return jnp.einsum('bsi,oi->bso', x, w) * s
        h = jax.nn.silu(_tlin(x, w1_w, w1_s)) * _tlin(x, w2_w, w2_s)
        h = jax.nn.gelu(_tlin(h, h1_w, h1_s), approximate=False)
        h = jax.nn.gelu(_tlin(h, h2_w, h2_s), approximate=False)
        return _tlin(h, w3_w, w3_s)
    x = L0_attn_query
    x = _layernorm(x + _L0_attn_ref(x, L0_attn_in_proj_w, L0_attn_in_proj_b, L0_attn_out_w, L0_attn_out_b, L0_attn_up_w, L0_attn_up_b), axis=-1)
    x = _layernorm(x + _L0_ffn_ref(x, L0_ffn_w1_w, L0_ffn_w1_s, L0_ffn_w2_w, L0_ffn_w2_s, L0_ffn_h1_w, L0_ffn_h1_s, L0_ffn_h2_w, L0_ffn_h2_s, L0_ffn_w3_w, L0_ffn_w3_s), axis=-1)
    return x

_drawn_inputs = setup_inputs


def setup_inputs(seed=0):
    import zlib

    import numpy as np

    out = dict(_drawn_inputs(seed))
    spreads = {'L0_attn_in_proj_b': (0.0, 0.1), 'L0_attn_out_b': (0.0, 0.1), 'L0_attn_up_b': (0.0, 0.1)}
    factors = {'L0_attn_in_proj_w': 8.0,
     'L0_ffn_w1_w': 8.0,
     'L0_ffn_w1_s': 8.0,
     'L0_ffn_w2_w': 8.0,
     'L0_ffn_w2_s': 8.0,
     'L0_ffn_h1_w': 8.0,
     'L0_ffn_h1_s': 8.0,
     'L0_ffn_h2_w': 8.0,
     'L0_ffn_h2_s': 8.0,
     'L0_ffn_w3_w': 8.0,
     'L0_ffn_w3_s': 8.0}
    for name, (base, spread) in spreads.items():
        noise = np.random.default_rng([zlib.crc32(name.encode()), seed]).standard_normal(out[name].shape)
        drawn = base * np.exp(spread * noise) if base else spread * noise
        out[name] = jnp.asarray(drawn.astype(out[name].dtype))
    for name, factor in factors.items():
        out[name] = (out[name] * factor).astype(out[name].dtype)
    return out
```

```python
import numpy as np
import concourse.bass as bass
from concourse import mybir
from contextlib import ExitStack

F32, F32R, BF16 = mybir.dt.float32, mybir.dt.float32r, mybir.dt.bfloat16
ALU, ACT, AX = mybir.AluOpType, mybir.ActivationFunctionType, mybir.AxisListType

B, S0, E = 8, 1024, 256
H, HD, LEVELS = 16, 16, 4
HG = 4
G = H // HG
DH = 1024
EPS = 1e-5
K_PIECES = (0, 0, 0, 1, 1, 2)
Q_PIECES = (0, 1, 2, 0, 1, 0)
ROWS = 16 * len(K_PIECES)
WQK, WV, WO, WUP = 0, 1024, 1536, 2560
WCOLS = 3072
CBQK, CBO, CBUP, CBV, CBOB, CBUPB = 0, 4, 6, 8, 264, 520
CCOLS = 776


def token_order():
    order = np.arange(S0 >> (LEVELS - 1))
    for _ in range(LEVELS - 1):
        order = np.concatenate([2 * order, 2 * order + 1])
    return order


def shifted(n, by):
    order = np.arange(S0 >> (LEVELS - 1))
    while len(order) < n:
        order = np.concatenate([2 * order, 2 * order + 1])
    at = np.argsort(order)
    src = at[np.clip(order + by, 0, n - 1)]
    runs, i = [], 0
    while i < n:
        k = 1
        while i + k < n and src[i + k] == src[i] + k:
            k += 1
        runs.append((i, int(src[i]), k))
        i += k
    return runs


def clear_semaphores(nc, signals):
    with nc.Block() as block:
        @block.sync
        def _(sp):
            for s in signals:
                sp.sem_clear(s.sem)


class Signal:

    def __init__(self, ctx, nc, name, per, step=1, lead=0):
        self.sem, self.per, self.step, self.lead = ctx.enter_context(nc.semaphore(name)), per, step, lead

    def at(self, b, n):
        return b * (self.per * self.step) + (n + self.lead) * self.step

    def wait(self, engine, b, n):
        value = self.at(b, n)
        if isinstance(b, int) and value <= 0:
            return
        engine.wait_ge(self.sem, value)


def attention_level(nc, lvl, xt, xtok, wpack, cpack, ident_in, scr, up_hi, up_lo, x1):
    S = S0 >> lvl
    T = S // 128
    W = min(512, S)
    NB = S // W
    NQ = W // 128
    U = G * NB
    STEPS = U * T
    MT = HG * NQ * NB
    MPS = MT // T
    PT = 4 * NB
    OT = T if lvl == 0 else 2 * NB
    below = lvl < LEVELS - 1
    mine, last_level = lvl, lvl == 0

    def proj(n):
        return (n // NB) % 2, n // (2 * NB), n % NB

    def unit(u):
        return u // NB, u % NB

    def plan(first, last):
        p = []
        if first:
            p += [("x",)] + [("proj", n) for n in range(PT)] + [("stack", 0), ("stack", 1)]
            p += [("max", 0, m) for m in range(MT)] + [("neg", 0)]
            p += [("v", t) for t in range(T)]
            return p
        if not last:
            p.append(("x",))
        if below and not last_level:
            p.append(("coarse",))
        tasks = [] if last else [("proj", n) for n in range(PT)]
        start = min(2, STEPS - PT)
        for s in range(STEPS):
            u, kt = divmod(s, T)
            p.append(("score", s))
            if not (last and u == U - 1):
                p += [("max", u + 1, kt * MPS + m) for m in range(MPS)]
            if s > 0:
                p.append(("value", s - 1))
                if s % T == 0:
                    p.append(("norm", u - 1))
            if u > 0 and kt == min(3, T - 1):
                p.append(("attn_hi", u - 1))
            if tasks and s >= start:
                p.append(tasks.pop(0))
            if kt == T - 1 and not (last and u == U - 1):
                p.append(("neg", u + 1))
            if not last and not tasks and ("stack", 0) not in p and s >= STEPS // 2:
                p.append(("stack", 0))
        p += [("value", STEPS - 1), ("norm", U - 1)]
        if not last:
            p += [("stack", 1)] + [("v", t) for t in range(T)]
        p.append(("attn_hi", U - 1))
        p += [("out", k) for k in range(OT)]
        if not last_level:
            p.append(("interp",))
        return p

    before, body, end = plan(True, False), plan(False, False), plan(False, True)
    if ("stack", 0) in body:
        need = body.index(("max", U, 0))
        if body.index(("stack", 0)) > need:
            body.remove(("stack", 0))
            need = body.index(("max", U, 0))
            body.insert(need, ("stack", 0))
    for q in (body,):
        tail_proj = max(q.index(("proj", n)) for n in range(PT // 2))
        assert q.index(("stack", 0)) > tail_proj
    AUX0 = sum(e[0] in ("proj", "neg") for e in before)
    AUX = sum(e[0] in ("proj", "neg") for e in body)

    with ExitStack() as ctx:
        def sb(name, shape, dt=F32):
            return ctx.enter_context(nc.sbuf_tensor(f"{name}{lvl}", shape, dt))

        def pb(name, shape):
            return ctx.enter_context(nc.psum_tensor(f"{name}{lvl}", shape, F32))

        signals = []

        def sig(name, per, step=1, lead=0):
            signals.append(Signal(ctx, nc, f"{name}_{lvl}", per, step, lead))
            return signals[-1]

        w_hi, w_lo = sb("w_hi", [128, WCOLS], F32R), sb("w_lo", [128, WCOLS], F32R)
        consts = sb("consts", [128, CCOLS])
        ident = sb("ident", [128, 128])
        x_in = sb("x_in", [128, S])
        x_hi, x_lo = sb("x_hi", [128, 2, S], F32R), sb("x_lo", [128, 2, S], F32R)
        qk = sb("qk", [128, W])
        qk_rest = sb("qk_rest", [128, W])
        qk_bf = sb("qk_bf", [128, 2, 3, W], BF16)
        k_st = sb("k_st", [128, H, S], BF16)
        q_st = sb("q_st", [128, H, S], BF16)
        v_aug = sb("v_aug", [128, T, H, 32])
        probs = sb("probs", [128, 2, HG, W])
        part_max = sb("part_max", [128, 2, NQ * HG, NB])
        row_max = sb("row_max", [128, 2, NQ, HG])
        neg_f = sb("neg_f", [HG, W])
        neg_bf = sb("neg_bf", [HG, 2, 2, W], BF16)
        raw = sb("raw", [128, W])
        attn = sb("attn", [128, 2, W])
        a_hi, a_lo = sb("a_hi", [128, G, S], F32R), sb("a_lo", [128, G, S], F32R)
        bias_o = sb("bias_o", [128, 2])
        if last_level:
            up_ring_hi, up_ring_lo = sb("up_ring_hi", [128, 2, 2, 128], F32R), sb("up_ring_lo", [128, 2, 2, 128], F32R)
            xt_ring = sb("xt_ring", [128, 2, E])
            s_ring = sb("s_ring", [128, 2, E])
            bias_row = consts[:, CBOB:CBOB + E]
            stats = sb("stats", [128, 2, 6])
            moments = sb("moments", [128, 2, 2])
            var_eps = sb("var_eps", [128, 2])
            rstd = sb("rstd", [128, 2])
            minus_half = sb("minus_half", [128, 1])
        else:
            if below:
                c_hi, c_lo = sb("c_hi", [128, 2, S], F32R), sb("c_lo", [128, 2, S], F32R)
            cur = sb("cur", [128, 2, S])
            cur34 = sb("cur34", [128, 2, S])
            fine = sb("fine", [128, 2, 2 * S])
            fine_hi, fine_lo = sb("fine_hi", [128, 2, 2 * S], F32R), sb("fine_lo", [128, 2, 2 * S], F32R)

        w_stage = probs[:, :, :, :].rearrange("p a h w -> p (a h w)") if WCOLS <= 2 * HG * W else sb("w_stage", [128, WCOLS])

        p_s = pb("p_s", [128, 4, 512])
        p_m = pb("p_m", [128, 2, 512])
        p_o = pb("p_o", [128, 512])
        p_a = pb("p_a", [128, 512])

        w_in_done = sig("w_in_done", 0, 16)
        w_hi_done, w_lo_done = sig("w_hi_done", 0), sig("w_lo_done", 0)
        const_done, set_done = sig("const_done", 0), sig("set_done", 0)
        x_loaded = sig("x_loaded", 2, 16)
        x_hi_done, x_lo_done = sig("x_hi_done", 2), sig("x_lo_done", 2)
        aux_mm = sig("aux_mm", 0)
        aux_read = sig("aux_read", 0)
        qk_rest_done = sig("qk_rest_done", PT)
        qk_b = sig("qk_b", PT)
        qk_c = sig("qk_c", PT)
        stored = [sig(f"stored{i}", PT // 2, 16) for i in range(2)]
        stacked = [sig(f"stacked{m}", 2 * len(K_PIECES), 16) for m in range(2)]
        v_mm, v_done = sig("v_mm", T), sig("v_done", T)
        max_mm, max_read = sig("max_mm", U * MT), sig("max_read", U * MT)
        max_done = sig("max_done", U)
        neg_b = sig("neg_b", U, lead=1)
        neg_placed = sig("neg_placed", U, 32, lead=1)
        score_mm = sig("score_mm", 2 * STEPS)
        exp_done = sig("exp_done", 2 * STEPS, lead=2)
        value_mm = sig("value_mm", STEPS, lead=2)
        raw_done = sig("raw_done", U, lead=1)
        den_done, rec_done, attn_done = sig("den_done", U, lead=2), sig("rec_done", U, lead=2), sig("attn_done", U, lead=2)
        a_hi_done, a_lo_done = sig("a_hi_done", U, lead=2), sig("a_lo_done", U, lead=2)
        out_mm, out_read = sig("out_mm", OT, lead=2), sig("out_read", OT, lead=2)
        if last_level:
            up_loaded = [sig(f"up_loaded{i}", OT // 2, 32) for i in range(2)]
            xt_loaded = [sig(f"xt_loaded{i}", OT // 2, 16) for i in range(2)]
            xt_biased = sig("xt_biased", OT, lead=2)
            stats_done, moments_done = sig("stats_done", OT), sig("moments_done", OT)
            eps_done, rstd_done = sig("eps_done", OT), sig("rstd_done", OT)
            y_done = sig("y_done", OT, lead=2)
            y_stored = [sig(f"y_stored{i}", OT // 2, 16, lead=1) for i in range(2)]
        else:
            c_loaded = sig("c_loaded", 1, 32)
            cur34_done, fine_done = sig("cur34_done", 1), sig("fine_done", 1, lead=1)
            fine_hi_done, fine_lo_done = sig("fine_hi_done", 1, lead=1), sig("fine_lo_done", 1, lead=1)
            fine_stored = sig("fine_stored", 1, 32, lead=1)
        held = sig("held", 0)

        def batches(engine, steps):
            steps(before, None, 0)
            with engine.Fori(0, B - 1) as i:
                steps(body, i, i * AUX + AUX0)
            steps(end, B - 1, (B - 1) * AUX + AUX0)

        def target(b, u):
            if b is None:
                return 0, 0
            return (b + 1, 0) if u == U else (b, u)

        def following(b):
            return 0 if b is None else b + 1

        def tail_slot(pl, k):
            return (k + (T if any(e[0] == "v" for e in pl) else 0)) % 4

        def tail_ready(engine, pl, b, k):
            has_v = any(e[0] == "v" for e in pl)
            n = k - 4
            if n < 0:
                return
            if has_v and n < T:
                v_done.wait(engine, following(b), n + 1)
            else:
                out_read.wait(engine, b, n - (T if has_v else 0) + 1)

        with nc.Block() as block:
            @block.sync
            def _(sp):
                def hold():
                    sp.sem_inc(held.sem, 1)

                sp.dma_start(w_stage[:, 0:WCOLS], wpack[lvl, :, :]).then_inc(w_in_done.sem, 16)
                sp.dma_start(consts[:, :], cpack[lvl, :, :]).then_inc(w_in_done.sem, 16)
                sp.dma_start(ident[:, :], ident_in).then_inc(w_in_done.sem, 16)

                def steps(pl, b, aux):
                    nb = following(b)
                    for e in pl:
                        kind = e[0]
                        if kind == "x":
                            for c in range(2):
                                if b is not None or c > 0:
                                    x_lo_done.wait(sp, nb, c)
                                    hold()
                                sp.dma_start(x_in[:, :], xt[nb, c * 128:(c + 1) * 128, 0:S]).then_inc(x_loaded.sem, 16)
                        elif kind == "coarse":
                            out_mm.wait(sp, b, 0)
                            hold()
                            sp.dma_start(c_hi[:, :, :].bitcast(F32), up_hi[lvl][b, :, :].rearrange("(c p) t -> p c t", p=128))\
                              .then_inc(c_loaded.sem, 16)
                            sp.dma_start(c_lo[:, :, :].bitcast(F32), up_lo[lvl][b, :, :].rearrange("(c p) t -> p c t", p=128))\
                              .then_inc(c_loaded.sem, 16)
                        elif kind == "proj":
                            t, m, blk = proj(e[1])
                            qk_c.wait(sp, nb, e[1] + 1)
                            hold()
                            if b is not None:
                                stacked[m].wait(sp, b, 2 * len(K_PIECES))
                                hold()
                            sp.dma_start(scr[t, :, m * 128:(m + 1) * 128, blk * W:(blk + 1) * W].rearrange("i p t -> p i t"),
                                         qk_bf[:, e[1] % 2, :, :]).then_inc(stored[e[1] % 2].sem, 16)
                        elif kind == "stack":
                            m = e[1]
                            for i in range(2):
                                stored[i].wait(sp, nb, (m + 1) * NB)
                                hold()
                            if b is not None:
                                score_mm.wait(sp, b, (m + 1) * STEPS)
                                hold()
                            for r in range(len(K_PIECES)):
                                for t, st, pieces in ((0, q_st, Q_PIECES), (1, k_st, K_PIECES)):
                                    sp.dma_start(st[16 * r:16 * r + 16, 8 * m:8 * m + 8, :],
                                                 scr[t, pieces[r], m * 128:(m + 1) * 128, 0:S].rearrange("(h d) t -> d h t", d=16))\
                                      .then_inc(stacked[m].sem, 16)
                        elif kind == "neg":
                            tb, u = target(b, e[1])
                            g, blk = unit(u)
                            neg_b.wait(sp, tb, u + 1)
                            hold()
                            for i in range(2):
                                sp.dma_start(q_st[ROWS + i:ROWS + i + 1, HG * g:HG * g + HG, blk * W:(blk + 1) * W],
                                             neg_bf[0:HG, u % 2, i, :]).then_inc(neg_placed.sem, 16)
                        elif kind == "out" and last_level:
                            k = e[1]
                            out_mm.wait(sp, b, k - 1)
                            hold()
                            for src, dst in ((up_hi, up_ring_hi), (up_lo, up_ring_lo)):
                                sp.dma_start(dst[:, k % 2, :, :].bitcast(F32),
                                             src[0][b, :, k * 128:(k + 1) * 128].rearrange("(c p) t -> p c t", p=128))\
                                  .then_inc(up_loaded[k % 2].sem, 16)
                            xt_biased.wait(sp, b, k - 1)
                            hold()
                            sp.dma_start(xt_ring[:, k % 2, :], xtok[b, k * 128:(k + 1) * 128, :])\
                              .then_inc(xt_loaded[k % 2].sem, 16)
                            if k >= 2:
                                store_y(b, k - 2)
                            if k == OT - 1:
                                store_y(b, k - 1)
                                store_y(b, k)
                        elif kind == "interp":
                            fine_hi_done.wait(sp, b, 1)
                            hold()
                            sp.dma_start(up_hi[lvl - 1][b, :, :].rearrange("(c p) t -> p c t", p=128), fine_hi[:, :, :].bitcast(F32))\
                              .then_inc(fine_stored.sem, 16)
                            fine_lo_done.wait(sp, b, 1)
                            hold()
                            sp.dma_start(up_lo[lvl - 1][b, :, :].rearrange("(c p) t -> p c t", p=128), fine_lo[:, :, :].bitcast(F32))\
                              .then_inc(fine_stored.sem, 16)

                def store_y(b, k):
                    y_done.wait(sp, b, k + 1)
                    hold()
                    sp.dma_start(x1[b, k * 128:(k + 1) * 128, :], s_ring[:, k % 2, :]).then_inc(y_stored[k % 2].sem, 16)

                if last_level:
                    for i in range(2):
                        sp.sem_inc(y_stored[i].sem, 16)
                else:
                    sp.sem_inc(fine_stored.sem, 32)
                sp.sem_inc(neg_placed.sem, 32)
                batches(sp, steps)
                if last_level:
                    for i in range(2):
                        sp.wait_ge(y_stored[i].sem, y_stored[i].at(B - 1, OT // 2))
                else:
                    sp.wait_ge(fine_stored.sem, fine_stored.at(B - 1, 1))
                for i in range(2):
                    sp.wait_ge(stored[i].sem, stored[i].at(B - 1, PT // 2))

            @block.gpsimd
            def _(pool):
                pool.memset(v_aug[:, :, :, HD + 1:32], 0.0).then_inc(set_done.sem, 1)
                pool.wait_ge(set_done.sem, 1)
                pool.memset(v_aug[:, :, :, HD:HD + 1], 1.0).then_inc(set_done.sem, 1)
                pool.wait_ge(set_done.sem, 2)
                pool.memset(k_st[ROWS:ROWS + 2, :, :], 1.0).then_inc(set_done.sem, 1)
                pool.wait_ge(set_done.sem, 3)
                if last_level:
                    pool.memset(minus_half[:, :], -0.5).then_inc(set_done.sem, 1)
                    pool.wait_ge(set_done.sem, 4)
                pool.sem_inc(a_lo_done.sem, 2)
                pool.sem_inc(neg_b.sem, 1)

                def steps(pl, b, aux):
                    nb = following(b)
                    k_aux = 0
                    for e in pl:
                        kind = e[0]
                        if kind == "x":
                            for c in range(2):
                                x_hi_done.wait(pool, nb, c + 1)
                                if b is not None:
                                    v_mm.wait(pool, b, T)
                                pool.tensor_tensor(out=x_lo[:, c, :], in0=x_in[:, :], in1=x_hi[:, c, :], op=ALU.subtract)\
                                    .then_inc(x_lo_done.sem, 1)
                        elif kind == "proj":
                            n = e[1]
                            bf = qk_bf[:, n % 2, :, :]
                            k_aux += 1
                            pool.wait_ge(aux_read.sem, aux + k_aux)
                            if b is not None or n > 0:
                                qk_c.wait(pool, nb, n)
                            pool.tensor_tensor(out=qk_rest[:, :], in0=qk[:, :], in1=bf[:, 0, :], op=ALU.subtract)\
                                .then_inc(qk_rest_done.sem, 1)
                            qk_rest_done.wait(pool, nb, n + 1)
                            pool.sem_inc(held.sem, 1)
                            pool.tensor_copy(bf[:, 1, :], qk_rest[:, :]).then_inc(qk_b.sem, 1)
                            qk_b.wait(pool, nb, n + 1)
                            pool.tensor_tensor(out=bf[:, 2, :], in0=qk_rest[:, :], in1=bf[:, 1, :], op=ALU.subtract)\
                                .then_inc(qk_c.sem, 1)
                        elif kind == "neg":
                            tb, u = target(b, e[1])
                            k_aux += 1
                            pool.wait_ge(aux_read.sem, aux + k_aux)
                            pool.tensor_tensor(out=neg_bf[:, u % 2, 1, :], in0=neg_f[:, :],
                                               in1=neg_bf[:, u % 2, 0, :], op=ALU.subtract).then_inc(neg_b.sem, 1)
                        elif kind == "attn_hi":
                            u = e[1]
                            g, blk = unit(u)
                            a_hi_done.wait(pool, b, u + 1)
                            pool.tensor_tensor(out=a_lo[:, g, blk * W:(blk + 1) * W], in0=attn[:, u % 2, :],
                                               in1=a_hi[:, g, blk * W:(blk + 1) * W], op=ALU.subtract)\
                                .then_inc(a_lo_done.sem, 1)
                        elif kind == "out" and last_level:
                            k = e[1]
                            eps_done.wait(pool, b, k + 1)
                            pool.tensor_tensor(out=rstd[:, k % 2:k % 2 + 1], in0=var_eps[:, k % 2:k % 2 + 1],
                                               in1=minus_half[:, :], op=ALU.pow).then_inc(rstd_done.sem, 1)
                        elif kind == "interp":
                            fine_hi_done.wait(pool, b, 1)
                            fine_stored.wait(pool, b, 0)
                            pool.tensor_tensor(out=fine_lo[:, :, :], in0=fine[:, :, :], in1=fine_hi[:, :, :], op=ALU.subtract)\
                                .then_inc(fine_lo_done.sem, 1)

                if not last_level:
                    pool.sem_inc(fine_lo_done.sem, 1)
                batches(pool, steps)

            @block.scalar
            def _(act):
                act.wait_ge(w_in_done.sem, 48)
                act.activation(w_hi[:, :], w_stage[:, 0:WCOLS], ACT.Copy).then_inc(w_hi_done.sem, 1)
                for s, n in ((exp_done, 2), (raw_done, 1), (a_hi_done, 2)):
                    act.sem_inc(s.sem, n)
                if not last_level:
                    act.sem_inc(fine_hi_done.sem, 1)
                    act.sem_inc(out_read.sem, 2)

                def steps(pl, b, aux):
                    nb = following(b)
                    k_aux = k_tail = 0
                    for e in pl:
                        kind = e[0]
                        if kind == "x":
                            for c in range(2):
                                x_loaded.wait(act, nb, c + 1)
                                if b is not None:
                                    v_mm.wait(act, b, T)
                                act.activation(x_hi[:, c, :], x_in[:, :], ACT.Copy).then_inc(x_hi_done.sem, 1)
                        elif kind == "proj":
                            n = e[1]
                            t, m, blk = proj(n)
                            col = CBQK + 2 * t + m
                            act.wait_ge(aux_mm.sem, aux + k_aux + 1)
                            if b is not None or n >= 1:
                                qk_rest_done.wait(act, nb, n)
                            if b is not None or n >= 2:
                                stored[n % 2].wait(act, nb, n // 2)
                            act.activation(qk[:, :], p_a[:, 0:W], ACT.Identity, bias=consts[:, col:col + 1])
                            act.activation(qk_bf[:, n % 2, 0, :], p_a[:, 0:W], ACT.Identity, bias=consts[:, col:col + 1])\
                               .then_inc(aux_read.sem, 1)
                            k_aux += 1
                        elif kind == "neg":
                            tb, u = target(b, e[1])
                            act.wait_ge(aux_mm.sem, aux + k_aux + 1)
                            if b is not None:
                                neg_b.wait(act, tb, u)
                                neg_placed.wait(act, tb, u - 1)
                            act.activation(neg_f[:, :], p_a[0:HG, 0:W], ACT.Copy, scale=-1.0)
                            act.activation(neg_bf[:, u % 2, 0, :], p_a[0:HG, 0:W], ACT.Copy, scale=-1.0).then_inc(aux_read.sem, 1)
                            k_aux += 1
                        elif kind == "score":
                            s = e[1]
                            for p in range(2):
                                score_mm.wait(act, b, 2 * s + p + 1)
                                value_mm.wait(act, b, s - 1)
                                act.activation(probs[:, s % 2, 2 * p:2 * p + 2, :], p_s[:, 2 * p:2 * p + 2, 0:W], ACT.Exp,
                                               scale=HD ** -0.5).then_inc(exp_done.sem, 1)
                        elif kind == "norm":
                            u = e[1]
                            value_mm.wait(act, b, (u + 1) * T)
                            attn_done.wait(act, b, u)
                            act.activation(raw[:, :], p_o[:, 0:W], ACT.Copy).then_inc(raw_done.sem, 1)
                        elif kind == "attn_hi":
                            u = e[1]
                            g, blk = unit(u)
                            attn_done.wait(act, b, u + 1)
                            out_mm.wait(act, b, 0)
                            act.activation(a_hi[:, g, blk * W:(blk + 1) * W], attn[:, u % 2, :], ACT.Copy)\
                               .then_inc(a_hi_done.sem, 1)
                        elif kind == "out" and not last_level:
                            k = e[1]
                            m, blk = k // NB, k % NB
                            out_mm.wait(act, b, k + 1)
                            fine_done.wait(act, b, 0)
                            act.activation(cur[:, m, blk * W:(blk + 1) * W], p_s[:, tail_slot(pl, k), 0:W], ACT.Identity,
                                           bias=bias_o[:, m:m + 1]).then_inc(out_read.sem, 1)
                        elif kind == "interp":
                            fine_done.wait(act, b, 1)
                            fine_stored.wait(act, b, 0)
                            act.activation(fine_hi[:, :, :], fine[:, :, :], ACT.Copy).then_inc(fine_hi_done.sem, 1)

                act.wait_ge(const_done.sem, 1)
                batches(act, steps)

            @block.vector
            def _(dve):
                dve.wait_ge(w_in_done.sem, 48)
                dve.wait_ge(w_hi_done.sem, 1)
                dve.tensor_tensor(out=w_lo[:, :], in0=w_stage[:, 0:WCOLS], in1=w_hi[:, :], op=ALU.subtract)\
                   .then_inc(w_lo_done.sem, 1)
                if last_level:
                    dve.tensor_tensor(out=bias_row, in0=consts[:, CBOB:CBOB + E], in1=consts[:, CBUPB:CBUPB + E],
                                      op=ALU.add).then_inc(const_done.sem, 1)
                else:
                    dve.tensor_tensor(out=bias_o[:, :], in0=consts[:, CBO:CBO + 2], in1=consts[:, CBUP:CBUP + 2],
                                      op=ALU.add).then_inc(const_done.sem, 1)
                for s in (den_done, rec_done, attn_done):
                    dve.sem_inc(s.sem, 2)
                if last_level:
                    dve.sem_inc(xt_biased.sem, 2)
                    dve.sem_inc(out_read.sem, 2)
                    dve.sem_inc(y_done.sem, 2)
                else:
                    dve.sem_inc(fine_done.sem, 1)
                dve.wait_ge(const_done.sem, 1)

                def finish_y(b, k):
                    rstd_done.wait(dve, b, k + 1)
                    dve.tensor_scalar(s_ring[:, k % 2, :], s_ring[:, k % 2, :], moments[:, k % 2, 0:1],
                                      rstd[:, k % 2:k % 2 + 1], ALU.subtract, ALU.mult).then_inc(y_done.sem, 1)

                def steps(pl, b, aux):
                    nb = following(b)
                    for e in pl:
                        kind = e[0]
                        if kind == "max":
                            tb, u = target(b, e[1])
                            m = e[2]
                            max_mm.wait(dve, tb, u * MT + m + 1)
                            if m == 0 and not (b is None):
                                neg_b.wait(dve, tb, u - 1)
                            col = m // NB
                            out = part_max[:, u % 2, col, m % NB:m % NB + 1] if NB > 1 else \
                                row_max[:, u % 2, col // HG, col % HG:col % HG + 1]
                            ins = dve.reduce_max(out, p_m[:, m % 2, 0:W], AX.X)
                            ins.then_inc(max_read.sem, 1)
                        elif kind == "neg" and NB > 1:
                            tb, u = target(b, e[1])
                            max_read.wait(dve, tb, (u + 1) * MT)
                            dve.tensor_tensor(out=row_max[:, u % 2, :, :].rearrange("p a h -> p (a h)"),
                                              in0=part_max[:, u % 2, :, 0], in1=part_max[:, u % 2, :, 1], op=ALU.max)\
                               .then_inc(max_done.sem, 1)
                        elif kind == "v":
                            t = e[1]
                            v_mm.wait(dve, nb, t + 1)
                            if b is not None:
                                value_mm.wait(dve, b, STEPS)
                            dve.tensor_tensor(out=v_aug[:, t, :, 0:HD],
                                              in0=p_s[:, t % 4, 0:E].rearrange("p (h d) -> p h d", d=HD),
                                              in1=consts[:, CBV:CBV + E].rearrange("p (h d) -> p h d", d=HD), op=ALU.add)\
                               .then_inc(v_done.sem, 1)
                        elif kind == "norm":
                            u = e[1]
                            raw_done.wait(dve, b, u + 1)
                            a_lo_done.wait(dve, b, u - 1)
                            den = attn[:, u % 2, :]
                            dve.sem_inc(held.sem, 1)
                            dve.stream_shuffle(den, raw[:, :], [HD] * 32).then_inc(den_done.sem, 1)
                            den_done.wait(dve, b, u + 1)
                            dve.reciprocal(den, den).then_inc(rec_done.sem, 1)
                            rec_done.wait(dve, b, u + 1)
                            dve.tensor_tensor(out=attn[:, u % 2, :], in0=raw[:, :], in1=den, op=ALU.mult)\
                               .then_inc(attn_done.sem, 1)
                        elif kind == "out" and last_level:
                            k = e[1]
                            xt_loaded[k % 2].wait(dve, b, k // 2 + 1)
                            y_stored[k % 2].wait(dve, b, k // 2)
                            dve.tensor_tensor(out=s_ring[:, k % 2, :], in0=xt_ring[:, k % 2, :], in1=bias_row, op=ALU.add)\
                               .then_inc(xt_biased.sem, 1)
                            out_mm.wait(dve, b, k + 1)
                            xt_biased.wait(dve, b, k + 1)
                            dve.tensor_tensor(out=s_ring[:, k % 2, :], in0=p_s[:, tail_slot(pl, k), 0:E], in1=s_ring[:, k % 2, :],
                                              op=ALU.add).then_inc(out_read.sem, 1)
                            out_read.wait(dve, b, k + 1)
                            dve.bn_stats(stats[:, k % 2, :], s_ring[:, k % 2, :]).then_inc(stats_done.sem, 1)
                            stats_done.wait(dve, b, k + 1)
                            dve.sem_inc(held.sem, 1)
                            dve.bn_aggr(moments[:, k % 2, :], stats[:, k % 2, :]).then_inc(moments_done.sem, 1)
                            moments_done.wait(dve, b, k + 1)
                            dve.tensor_scalar(var_eps[:, k % 2:k % 2 + 1], moments[:, k % 2, 1:2], EPS, None, ALU.add)\
                               .then_inc(eps_done.sem, 1)
                            if k > 0:
                                finish_y(b, k - 1)
                            if k == OT - 1:
                                finish_y(b, k)
                        elif kind == "interp":
                            out_read.wait(dve, b, OT)
                            fine_lo_done.wait(dve, b, 0)
                            dve.tensor_scalar(cur34[:, :, :], cur[:, :, :], 0.75, None, ALU.mult).then_inc(cur34_done.sem, 1)
                            cur34_done.wait(dve, b, 1)
                            runs = [(0, r) for r in shifted(S, -1)] + [(S, r) for r in shifted(S, 1)]
                            for at, (dst, src, n) in runs:
                                ins = dve.scalar_tensor_tensor(out=fine[:, :, at + dst:at + dst + n], in0=cur[:, :, src:src + n],
                                                               scalar=0.25, in1=cur34[:, :, dst:dst + n],
                                                               op0=ALU.mult, op1=ALU.add)
                            ins.then_inc(fine_done.sem, 1)

                batches(dve, steps)

            @block.tensor
            def _(pe):
                pe.wait_ge(w_hi_done.sem, 1)
                pe.wait_ge(w_lo_done.sem, 1)
                pe.wait_ge(set_done.sem, 3)
                pe.sem_inc(value_mm.sem, 2)
                pe.sem_inc(out_mm.sem, 2)

                def three(out, pairs):
                    terms = [t for (a_h, a_l), (b_h, b_l) in pairs for t in ((a_h, b_h), (a_l, b_h), (a_h, b_l))]
                    for n, (a, c) in enumerate(terms):
                        ins = pe.matmul(out, a, c, start=n == 0, stop=n == len(terms) - 1)
                    return ins

                def steps(pl, b, aux):
                    nb = following(b)
                    k_aux = k_tail = 0
                    for e in pl:
                        kind = e[0]
                        if kind == "proj":
                            t, m, blk = proj(e[1])
                            x_hi_done.wait(pe, nb, 2)
                            x_lo_done.wait(pe, nb, 2)
                            aux_free(b, aux, k_aux)
                            cols = [slice(WQK + c * 512 + t * 256 + m * 128, WQK + c * 512 + t * 256 + m * 128 + 128) for c in range(2)]
                            tok = slice(blk * W, (blk + 1) * W)
                            three(p_a[:, 0:W], [((w_hi[:, cols[c]], w_lo[:, cols[c]]), (x_hi[:, c, tok], x_lo[:, c, tok]))
                                                for c in range(2)]).then_inc(aux_mm.sem, 1)
                            k_aux += 1
                        elif kind == "neg":
                            tb, u = target(b, e[1])
                            if NB > 1:
                                max_done.wait(pe, tb, u + 1)
                            else:
                                max_read.wait(pe, tb, (u + 1) * MT)
                            aux_free(b, aux, k_aux)
                            for q in range(NQ):
                                ins = pe.transpose(p_a[0:HG, q * 128:(q + 1) * 128], row_max[:, u % 2, q, :], ident[:, :])
                            ins.then_inc(aux_mm.sem, 1)
                            k_aux += 1
                        elif kind == "v":
                            t = e[1]
                            x_hi_done.wait(pe, nb, 2)
                            x_lo_done.wait(pe, nb, 2)
                            tail_ready(pe, pl, b, k_tail)
                            tok = slice(t * 128, (t + 1) * 128)
                            wc = [slice(WV + c * 256, WV + (c + 1) * 256) for c in range(2)]
                            three(p_s[:, k_tail % 4, 0:E], [((x_hi[:, c, tok], x_lo[:, c, tok]), (w_hi[:, wc[c]], w_lo[:, wc[c]]))
                                                            for c in range(2)]).then_inc(v_mm.sem, 1)
                            k_tail += 1
                        elif kind == "out":
                            k = e[1]
                            a_hi_done.wait(pe, b, U)
                            a_lo_done.wait(pe, b, U)
                            tail_ready(pe, pl, b, k_tail)
                            if last_level:
                                tok = slice(k * 128, (k + 1) * 128)
                                up_loaded[k % 2].wait(pe, b, k // 2 + 1)
                                pairs = [((a_hi[:, g, tok], a_lo[:, g, tok]),
                                          (w_hi[:, WO + g * E:WO + (g + 1) * E], w_lo[:, WO + g * E:WO + (g + 1) * E])) for g in range(G)]
                                pairs += [((up_ring_hi[:, k % 2, c, :], up_ring_lo[:, k % 2, c, :]),
                                           (w_hi[:, WUP + c * E:WUP + (c + 1) * E], w_lo[:, WUP + c * E:WUP + (c + 1) * E])) for c in range(2)]
                                three(p_s[:, k_tail % 4, 0:E], pairs).then_inc(out_mm.sem, 1)
                            else:
                                m, blk = k // NB, k % NB
                                tok = slice(blk * W, (blk + 1) * W)

                                def wcol(base, c):
                                    at = slice(base + c * E + m * 128, base + c * E + m * 128 + 128)
                                    return w_hi[:, at], w_lo[:, at]
                                pairs = [(wcol(WO, g), (a_hi[:, g, tok], a_lo[:, g, tok])) for g in range(G)]
                                if below:
                                    c_loaded.wait(pe, b, 1)
                                    pairs += [(wcol(WUP, c), (c_hi[:, c, tok], c_lo[:, c, tok])) for c in range(2)]
                                three(p_s[:, k_tail % 4, 0:W], pairs).then_inc(out_mm.sem, 1)
                            k_tail += 1
                        elif kind == "score":
                            s = e[1]
                            u, kt = divmod(s, T)
                            g, blk = unit(u)
                            if s == 0:
                                v_done.wait(pe, b, T)
                                out_read.wait(pe, b, 0)
                            if kt == 0:
                                stacked[g // 2].wait(pe, b, 2 * len(K_PIECES))
                                neg_placed.wait(pe, b, u + 1)
                            for p in range(2):
                                exp_done.wait(pe, b, 2 * s + p - 1)
                                for j in (2 * p, 2 * p + 1):
                                    ins = pe.matmul(p_s[:, j, 0:W], k_st[0:ROWS + 2, HG * g + j, kt * 128:(kt + 1) * 128],
                                                    q_st[0:ROWS + 2, HG * g + j, blk * W:(blk + 1) * W], start=True, stop=True)
                                ins.then_inc(score_mm.sem, 1)
                        elif kind == "max":
                            tb, u = target(b, e[1])
                            m = e[2]
                            g, blk = unit(u)
                            q, j, kb = m // (HG * NB), (m // NB) % HG, m % NB
                            if m == 0:
                                stacked[g // 2].wait(pe, tb, 2 * len(K_PIECES))
                            n = u * MT + m
                            if not (b is None and n < 2):
                                max_read.wait(pe, tb, n - 1)
                            pe.matmul(p_m[:, m % 2, 0:W], q_st[0:ROWS, HG * g + j, blk * W + q * 128:blk * W + (q + 1) * 128],
                                      k_st[0:ROWS, HG * g + j, kb * W:(kb + 1) * W], start=True, stop=True).then_inc(max_mm.sem, 1)
                        elif kind == "value":
                            s = e[1]
                            u, kt = divmod(s, T)
                            g, blk = unit(u)
                            exp_done.wait(pe, b, 2 * s + 2)
                            if kt == 0:
                                raw_done.wait(pe, b, u)
                            for j in range(HG):
                                ins = pe.matmul(p_o[32 * j:32 * j + 32, 0:W], v_aug[:, kt, HG * g + j, :], probs[:, s % 2, j, :],
                                                start=kt == 0, stop=kt == T - 1)
                            ins.then_inc(value_mm.sem, 1)

                def aux_free(b, aux, k):
                    if not (b is None and k == 0):
                        pe.wait_ge(aux_read.sem, aux + k)

                batches(pe, steps)

        clear_semaphores(nc, signals)


W1COLS, HCOLS = 512, 1024
USES = 24
W3AT = 8 * W1COLS + 16 * HCOLS
FCOLS = W3AT + 8 * E


def w_cols(v):
    return (v * W1COLS, W1COLS) if v < 8 else (8 * W1COLS + (v - 8) * HCOLS, HCOLS)


def ffn(nc, x1, wf, scales, s3row, ident_in, lo_scr, out):
    with ExitStack() as ctx:
        def sb(name, shape, dt=F32):
            return ctx.enter_context(nc.sbuf_tensor(f"f_{name}", shape, dt))

        signals = []

        def sig(name, per, step=1, lead=0):
            signals.append(Signal(ctx, nc, f"f_{name}", per, step, lead))
            return signals[-1]

        w_hi = sb("w_hi", [128, FCOLS], F32R)
        w3_lo = sb("w3_lo", [128, 8 * E], F32R)
        lo_ring = sb("lo_ring", [128, 3, HCOLS], F32R)
        xa = sb("xa", [128, 2, 4, E])
        xt_hi, xt_lo = sb("xt_hi", [128, 2, 512], F32R), sb("xt_lo", [128, 2, 512], F32R)
        h_hi, h_lo = sb("h_hi", [128, 2, 8, 512], F32R), sb("h_lo", [128, 2, 8, 512], F32R)
        gate = sb("gate", [128, 2, 512])
        h_f = sb("h_f", [128, 2, 512])
        sc = sb("sc", [128, 32])
        s3 = sb("s3", [128, E])
        ident = sb("ident", [128, 128])
        s_ring = sb("s_ring", [128, 2, E])
        stats, moments = sb("stats", [128, 2, 6]), sb("moments", [128, 2, 2])
        var_eps, rstd, minus_half = sb("var_eps", [128, 2]), sb("rstd", [128, 2]), sb("minus_half", [128, 1])
        p_h = ctx.enter_context(nc.psum_tensor("p_h", [128, 4, 512], F32))
        p_t = ctx.enter_context(nc.psum_tensor("p_t", [128, 2, 512], F32))
        p_y = ctx.enter_context(nc.psum_tensor("p_y", [128, 2, 512], F32))

        const_in, raw_in = sig("const_in", 0), [sig(f"raw_in{i}", 0) for i in range(2)]
        prep_hi, prep_lo = sig("prep_hi", 0), sig("prep_lo", 0)
        prep_stored = [sig(f"prep_stored{i}", 0) for i in range(3)]
        set_done = sig("set_done", 0)
        x_in = sig("x_in", 1, 16)
        t_mm, t_hi, t_lo = sig("t_mm", 2), sig("t_hi", 2), sig("t_lo", 2)
        lo_in = [sig(f"lo_in{i}", USES // 3, 16) for i in range(3)]
        h_mm = sig("h_mm", 32, lead=3)
        act_read = sig("act_read", 24, lead=4)
        gated = sig("gated", 8, lead=2)
        hi_done, lo_done = sig("hi_done", 24), sig("lo_done", 24, lead=2)
        y_mm, y_scaled, y_sum = sig("y_mm", 4, lead=1), sig("y_scaled", 4, lead=2), sig("y_sum", 4, lead=5)
        stats_done, moments_done = sig("stats_done", 4), sig("moments_done", 4)
        eps_done, rstd_done, y_done = sig("eps_done", 4), sig("rstd_done", 4), sig("y_done", 4)
        stored = [sig(f"stored{i}", 2, 16, lead=1) for i in range(2)]
        held = sig("held", 0)
        PREP = [w_cols(v) for v in range(USES)] + [(W3AT, HCOLS), (W3AT + HCOLS, HCOLS)]

        def bank(v, which=0):
            return 2 * v + which if v < 8 else 16 + v - 8

        def halves(engine, steps):
            with engine.Fori(0, B) as b:
                for half in range(2):
                    steps(b, half, b * 2 + half)

        with nc.Block() as block:
            @block.sync
            def _(sp):
                for dst, src in ((sc, scales), (s3, s3row), (ident, ident_in)):
                    sp.dma_start(dst[:, :], src).then_inc(const_in.sem, 16)
                def store_lo(engine, n):
                    engine.wait_ge(prep_lo.sem, n + 1)
                    col, k = PREP[n]
                    engine.dma_start(lo_scr[:, col:col + k], lo_ring[:, n % 3, 0:k].bitcast(F32)).then_inc(prep_stored[n % 3].sem, 16)

                for n, (col, k) in enumerate(PREP):
                    if n >= 2:
                        sp.wait_ge(prep_lo.sem, n - 1)
                    sp.dma_start(xa[:, n % 2, :, :].rearrange("p a e -> p (a e)")[:, 0:k], wf[:, col:col + k])\
                      .then_inc(raw_in[n % 2].sem, 16)
                    if 1 <= n <= USES:
                        store_lo(sp, n - 1)
                for i in range(3):
                    sp.wait_ge(prep_stored[i].sem, 16 * (USES // 3))
                sp.wait_ge(prep_lo.sem, len(PREP))

                def steps(b, half, hh):
                    y_sum.wait(sp, hh, -4)
                    sp.sem_inc(held.sem, 1)
                    sp.dma_start(xa[:, half, :, :], x1[b, half * 512:(half + 1) * 512, :].rearrange("(q p) e -> p q e", p=128))\
                      .then_inc(x_in.sem, 16)
                    for v in range(USES):
                        h_mm.wait(sp, hh, (bank(v - 3, 1 if v - 3 < 8 else 0) + 1) if v >= 3 else v - 2)
                        sp.sem_inc(held.sem, 1)
                        col, k = w_cols(v)
                        sp.dma_start(lo_ring[:, v % 3, 0:k].bitcast(F32), lo_scr[:, col:col + k]).then_inc(lo_in[v % 3].sem, 16)

                halves(sp, steps)

            @block.gpsimd
            def _(pool):
                pool.memset(minus_half[:, :], -0.5).then_inc(set_done.sem, 1)
                pool.wait_ge(set_done.sem, 1)
                def steps(b, half, hh):
                    for q in range(4):
                        eps_done.wait(pool, hh, q + 1)
                        pool.tensor_tensor(out=rstd[:, q % 2:q % 2 + 1], in0=var_eps[:, q % 2:q % 2 + 1],
                                           in1=minus_half[:, :], op=ALU.pow).then_inc(rstd_done.sem, 1)

                halves(pool, steps)

            @block.scalar
            def _(act):
                for n, (col, k) in enumerate(PREP):
                    act.wait_ge(raw_in[n % 2].sem, 16 * (n // 2 + 1))
                    act.activation(w_hi[:, col:col + k], xa[:, n % 2, :, :].rearrange("p a e -> p (a e)")[:, 0:k], ACT.Copy)\
                       .then_inc(prep_hi.sem, 1)
                act.wait_ge(const_in.sem, 48)
                act.sem_inc(act_read.sem, 4)
                for i in range(2):
                    act.sem_inc(stored[i].sem, 16)

                def steps(b, half, hh):
                    for c in range(2):
                        t_mm.wait(act, hh, c + 1)
                        act.activation(xt_hi[:, c, :], p_t[:, c, :], ACT.Copy).then_inc(t_hi.sem, 1)
                    for v in range(USES):
                        h_mm.wait(act, hh, bank(v) + 1)
                        if v < 8:
                            gated.wait(act, hh, v - 1)
                            act.activation(gate[:, v % 2, :], p_h[:, bank(v) % 4, :], ACT.Silu, scale=sc[:, v:v + 1])\
                               .then_inc(act_read.sem, 1)
                            gated.wait(act, hh, v + 1)
                        else:
                            lo_done.wait(act, hh, v - 1)
                            act.activation(h_f[:, v % 2, :], p_h[:, bank(v) % 4, :], ACT.Gelu, scale=sc[:, 8 + v:9 + v])\
                               .then_inc(act_read.sem, 1)
                            act_read.wait(act, hh, v + 1)
                        if v == 0:
                            y_mm.wait(act, hh, 0)
                        act.activation(h_hi[:, (v // 8) % 2, v % 8, :], h_f[:, v % 2, :], ACT.Copy).then_inc(hi_done.sem, 1)
                    for q in range(4):
                        y_done.wait(act, hh, q + 1)
                        row = half * 512 + q * 128
                        act.dma_start(out[b, row:row + 128, :], s_ring[:, q % 2, :]).then_inc(stored[q % 2].sem, 16)

                halves(act, steps)
                for i in range(2):
                    act.wait_ge(stored[i].sem, stored[i].at(2 * B - 1, 2))

            @block.vector
            def _(dve):
                for n, (col, k) in enumerate(PREP):
                    dve.wait_ge(prep_hi.sem, n + 1)
                    if n >= USES:
                        dst = w3_lo[:, (n - USES) * HCOLS:(n - USES + 1) * HCOLS]
                    else:
                        if n >= 3:
                            dve.wait_ge(prep_stored[n % 3].sem, 16 * (n // 3))
                        dst = lo_ring[:, n % 3, 0:k]
                    dve.tensor_tensor(out=dst, in0=xa[:, n % 2, :, :].rearrange("p a e -> p (a e)")[:, 0:k],
                                      in1=w_hi[:, col:col + k], op=ALU.subtract).then_inc(prep_lo.sem, 1)
                dve.wait_ge(const_in.sem, 48)
                for s, n in ((lo_done, 2), (y_scaled, 2), (y_sum, 5), (gated, 2)):
                    dve.sem_inc(s.sem, n)

                def finish(hh, q):
                    rstd_done.wait(dve, hh, q + 1)
                    dve.tensor_scalar(s_ring[:, q % 2, :], s_ring[:, q % 2, :], moments[:, q % 2, 0:1],
                                      rstd[:, q % 2:q % 2 + 1], ALU.subtract, ALU.mult).then_inc(y_done.sem, 1)

                def steps(b, half, hh):
                    for c in range(2):
                        t_hi.wait(dve, hh, c + 1)
                        dve.tensor_tensor(out=xt_lo[:, c, :], in0=p_t[:, c, :], in1=xt_hi[:, c, :], op=ALU.subtract)\
                           .then_inc(t_lo.sem, 1)
                    for v in range(USES):
                        if v < 8:
                            h_mm.wait(dve, hh, bank(v, 1) + 1)
                            act_read.wait(dve, hh, v + 1)
                            lo_done.wait(dve, hh, v - 1)
                            dve.scalar_tensor_tensor(out=h_f[:, v % 2, :], in0=p_h[:, bank(v, 1) % 4, :], scalar=sc[:, 8 + v:9 + v],
                                                     in1=gate[:, v % 2, :], op0=ALU.mult, op1=ALU.mult).then_inc(gated.sem, 1)
                        hi_done.wait(dve, hh, v + 1)
                        dve.tensor_tensor(out=h_lo[:, (v // 8) % 2, v % 8, :], in0=h_f[:, v % 2, :],
                                          in1=h_hi[:, (v // 8) % 2, v % 8, :], op=ALU.subtract).then_inc(lo_done.sem, 1)
                    for q in range(4):
                        y_mm.wait(dve, hh, q + 1)
                        stored[q % 2].wait(dve, hh, q // 2)
                        dve.tensor_tensor(out=s_ring[:, q % 2, :], in0=p_y[:, q % 2, 0:E], in1=s3[:, :], op=ALU.mult)\
                           .then_inc(y_scaled.sem, 1)
                        y_scaled.wait(dve, hh, q + 1)
                        dve.tensor_tensor(out=s_ring[:, q % 2, :], in0=s_ring[:, q % 2, :], in1=xa[:, half, q, :], op=ALU.add)\
                           .then_inc(y_sum.sem, 1)
                        y_sum.wait(dve, hh, q + 1)
                        dve.bn_stats(stats[:, q % 2, :], s_ring[:, q % 2, :]).then_inc(stats_done.sem, 1)
                        stats_done.wait(dve, hh, q + 1)
                        dve.sem_inc(held.sem, 1)
                        dve.bn_aggr(moments[:, q % 2, :], stats[:, q % 2, :]).then_inc(moments_done.sem, 1)
                        moments_done.wait(dve, hh, q + 1)
                        dve.tensor_scalar(var_eps[:, q % 2:q % 2 + 1], moments[:, q % 2, 1:2], EPS, None, ALU.add)\
                           .then_inc(eps_done.sem, 1)
                        if q > 0:
                            finish(hh, q - 1)
                    finish(hh, 3)

                halves(dve, steps)

            @block.tensor
            def _(pe):
                pe.wait_ge(prep_lo.sem, len(PREP))
                pe.wait_ge(const_in.sem, 48)
                pe.sem_inc(h_mm.sem, 3)
                pe.sem_inc(y_mm.sem, 1)

                def bank_free(hh, u):
                    p = u - 4
                    if 0 <= p < 16 and p % 2:
                        gated.wait(pe, hh, p // 2 + 1)
                    elif 0 <= p < 16:
                        act_read.wait(pe, hh, p // 2 + 1)
                    else:
                        act_read.wait(pe, hh, p + 1 if p < 0 else 8 + p - 16 + 1)

                def steps(b, half, hh):
                    x_in.wait(pe, hh, 1)
                    for c in range(2):
                        for q in range(4):
                            ins = pe.transpose(p_t[:, c, q * 128:(q + 1) * 128], xa[:, half, q, c * 128:(c + 1) * 128], ident[:, :])
                        ins.then_inc(t_mm.sem, 1)
                    t_lo.wait(pe, hh, 2)
                    for v in range(USES):
                        lo_in[v % 3].wait(pe, hh, v // 3 + 1)
                        col, _ = w_cols(v)
                        kinds = 2 if v < 8 else 1
                        chunks = 2 if v < 8 else 8
                        for which in range(kinds):
                            u = bank(v, which)
                            bank_free(hh, u)
                            for c in range(chunks):
                                at_c = (which * chunks + c) * 128
                                wh = w_hi[:, col + at_c:col + at_c + 128]
                                wl = lo_ring[:, v % 3, at_c:at_c + 128]
                                if v < 8:
                                    m_hi, m_lo = xt_hi[:, c, :], xt_lo[:, c, :]
                                else:
                                    src = (v // 8 - 1) % 2
                                    if v % 8 == 0:
                                        lo_done.wait(pe, hh, (v // 8 - 1) * 8 + c + 1)
                                    m_hi, m_lo = h_hi[:, src, c, :], h_lo[:, src, c, :]
                                o = p_h[:, u % 4, :]
                                pe.matmul(o, wh, m_hi, start=c == 0, stop=False)
                                pe.matmul(o, wl, m_hi, start=False, stop=False)
                                ins = pe.matmul(o, wh, m_lo, start=False, stop=c == chunks - 1)
                            ins.then_inc(h_mm.sem, 1)
                    for q in range(4):
                        tok = slice(q * 128, (q + 1) * 128)
                        y_scaled.wait(pe, hh, q - 1)
                        for c in range(8):
                            if q == 0:
                                lo_done.wait(pe, hh, 16 + c + 1)
                            o, at_c = p_y[:, q % 2, 0:E], c * E
                            wh, wl = w_hi[:, W3AT + at_c:W3AT + at_c + E], w3_lo[:, at_c:at_c + E]
                            pe.matmul(o, h_hi[:, 0, c, tok], wh, start=c == 0, stop=False)
                            pe.matmul(o, h_hi[:, 0, c, tok], wl, start=False, stop=False)
                            ins = pe.matmul(o, h_lo[:, 0, c, tok], wh, start=False, stop=c == 7)
                        ins.then_inc(y_mm.sem, 1)

                halves(pe, steps)


def program(nc, xt, xtok, wpack, cpack, wf, scales, s3row, ident, out):
    scr = nc.dram_tensor("qk_scratch", (2, 3, E, S0), BF16, kind="Internal").ap()
    up_hi = [nc.dram_tensor(f"up_hi{i}", (B, E, S0 >> i), F32, kind="Internal").ap() for i in range(LEVELS - 1)]
    up_lo = [nc.dram_tensor(f"up_lo{i}", (B, E, S0 >> i), F32, kind="Internal").ap() for i in range(LEVELS - 1)]
    x1 = nc.dram_tensor("x1", (B, S0, E), F32, kind="Internal").ap()
    lo_scr = nc.dram_tensor("w_lo_scratch", (128, FCOLS), F32, kind="Internal").ap()
    for lvl in reversed(range(LEVELS)):
        attention_level(nc, lvl, xt, xtok, wpack, cpack, ident, scr, up_hi, up_lo, x1)
    ffn(nc, x1, wf, scales, s3row, ident, lo_scr, out)


def kernel(**inputs):
    import concourse.bacc as bacc
    from concourse.bass_utils import run_bass_kernel_spmd as run

    a = {k: np.asarray(v) for k, v in inputs.items()}
    f = np.float32
    order = token_order()
    x = a["L0_attn_query"][:, order, :]
    iw, ib = a["L0_attn_in_proj_w"], a["L0_attn_in_proj_b"]

    def chunks(wt):
        return wt.reshape(-1, 128, wt.shape[1]).transpose(1, 0, 2).reshape(128, -1)

    wpack, cpack = np.zeros((LEVELS, 128, WCOLS), f), np.zeros((LEVELS, 128, CCOLS), f)
    for i in range(LEVELS):
        wpack[i, :, WQK:WV] = chunks(iw[i, :2 * E].T)
        wpack[i, :, WV:WO] = chunks(iw[i, 2 * E:].T)
        wo = np.zeros((H, 32, E), f)
        wo[:, :HD] = a["L0_attn_out_w"][i].T.reshape(H, HD, E)
        wpack[i, :, WO:WUP] = chunks(wo.reshape(H * 32, E))
        cpack[i, :, CBQK:CBO] = ib[i, :2 * E].reshape(4, 128).T
        cpack[i, :, CBO:CBUP] = a["L0_attn_out_b"][i].reshape(2, 128).T
        cpack[i, :, CBV:CBOB] = ib[i, 2 * E:]
        cpack[i, :, CBOB:CBUPB] = a["L0_attn_out_b"][i]
        if i < LEVELS - 1:
            wpack[i, :, WUP:] = chunks(a["L0_attn_up_w"][i].T)
            cpack[i, :, CBUP:CBV] = a["L0_attn_up_b"][i].reshape(2, 128).T
            cpack[i, :, CBUPB:] = a["L0_attn_up_b"][i]

    def tiles(*ws):
        return np.concatenate([chunks(w[m * 128:(m + 1) * 128].T) for m in range(8) for w in ws], axis=1)

    wf = np.concatenate([tiles(a["L0_ffn_w1_w"], a["L0_ffn_w2_w"]), tiles(a["L0_ffn_h1_w"]), tiles(a["L0_ffn_h2_w"]),
                         chunks(a["L0_ffn_w3_w"].T)], axis=1)
    scales = np.concatenate([a[f"L0_ffn_{n}_s"].reshape(8, 128).T for n in ("w1", "w2", "h1", "h2")], axis=1)
    arrays = {
        "xt": np.ascontiguousarray(x.transpose(0, 2, 1)), "xtok": np.ascontiguousarray(x), "wpack": wpack, "cpack": cpack,
        "wf": np.ascontiguousarray(wf), "scales": np.ascontiguousarray(scales),
        "s3row": np.ascontiguousarray(np.broadcast_to(a["L0_ffn_w3_s"], (128, E))), "ident": np.eye(128, dtype=f),
    }
    nc = bacc.Bacc("TRN2", target_bir_lowering=False, num_devices=1)
    args = [nc.dram_tensor(k, v.shape, mybir.dt.from_np(v.dtype), kind="ExternalInput").ap() for k, v in arrays.items()]
    args.append(nc.dram_tensor("y", (B, S0, E), F32, kind="ExternalOutput").ap())
    program(nc, *args)
    r = run(nc, [arrays], core_ids=[0])
    return r.results[0]["y"][:, np.argsort(order), :]
```

```python
import numpy as np
import concourse.bass as bass
from concourse import mybir
from contextlib import ExitStack

F32, F32R, BF16 = mybir.dt.float32, mybir.dt.float32r, mybir.dt.bfloat16
ALU, ACT, AX = mybir.AluOpType, mybir.ActivationFunctionType, mybir.AxisListType

B, S0, E = 8, 1024, 256
H, HD, LEVELS = 16, 16, 4
HG = 4
G = H // HG
DH = 1024
EPS = 1e-5
K_PIECES = (0, 0, 0, 1, 1, 2)
Q_PIECES = (0, 1, 2, 0, 1, 0)
ROWS = 16 * len(K_PIECES)
WQK, WV, WO, WUP = 0, 1024, 1536, 2560
WCOLS = 3072
CBQK, CBO, CBUP, CBV, CBOB, CBUPB = 0, 4, 6, 8, 264, 520
CCOLS = 776
D_MAX = (3, 3, 2, 1)
FRONT = ((-50.5, -44.5, 2.2), (-14.8, -12.5, 1.4), (-6.75, -6.4, .9), (-2.4, -2.35, .1))
CUT = (13.3, 9.3, 4.3, 3)


def token_order():
    order = np.arange(S0 >> (LEVELS - 1))
    for _ in range(LEVELS - 1):
        order = np.concatenate([2 * order, 2 * order + 1])
    return order


def shifted(n, by):
    order = np.arange(S0 >> (LEVELS - 1))
    while len(order) < n:
        order = np.concatenate([2 * order, 2 * order + 1])
    at = np.argsort(order)
    src = at[np.clip(order + by, 0, n - 1)]
    runs, i = [], 0
    while i < n:
        k = 1
        while i + k < n and src[i + k] == src[i] + k:
            k += 1
        runs.append((i, int(src[i]), k))
        i += k
    return runs


def clear_semaphores(nc, signals):
    with nc.Block() as block:
        @block.sync
        def _(sp):
            for s in signals:
                sp.sem_clear(s.sem)


class Signal:

    def __init__(self, ctx, nc, name, per, step=1, lead=0):
        self.sem, self.per, self.step, self.lead = ctx.enter_context(nc.semaphore(name)), per, step, lead

    def at(self, it, n):
        return it * (self.per * self.step) + (n + self.lead) * self.step

    def wait(self, engine, it, n):
        if isinstance(it, int):
            if self.at(it, n) > 0:
                engine.wait_ge(self.sem, self.at(it, n))
            return
        reg, k = it
        assert self.at(k, n) > 0, self.sem
        engine.wait_ge(self.sem, reg * (self.per * self.step) + self.at(k, n))

    def open(self, engine):
        engine.sem_inc(self.sem, self.lead * self.step)


def number(it):
    return it if isinstance(it, int) else it[0] + it[1]


def earlier(it):
    return it - 1 if isinstance(it, int) else (it[0], it[1] - 1)


def attention_level(nc, lvl, xt, xtok, wpack, cpack, ident_in, scr, up_hi, up_lo, x1):
    S = S0 >> lvl
    last_level = lvl == 0
    below = lvl < LEVELS - 1
    W = 512
    SEQ = max(1, W // S)
    N = B // SEQ
    C = SEQ * S
    T = S // 128
    NT = C // 128
    NB = C // W
    NQ = W // 128
    QS = min(S, W)
    QP = W // QS
    KB = S // QS
    U = G * NB
    STEPS = U * T
    MT = HG * NQ * KB // QP
    MPS = MT // T
    PT = 4 * NB
    OT = NT if last_level else 2
    NP = 2 if T >= 4 else 1
    XS = 1 if last_level else 2
    AHEAD = D_MAX[lvl]

    def proj(n):
        return (n // NB) % 2, n // (2 * NB), n % NB

    def unit(u):
        return u // NB, u % NB

    def timeline():
        p = []
        x_at, proj_at, proj_gap = FRONT[lvl]
        p.append((x_at, "x", 0))
        p += [(proj_at + proj_gap * n, "proj", n) for n in range(PT)]
        for g in range(G):
            p.append((max(proj_at + proj_gap * (2 * NB * (g // 2 + 1) - 1) + .01, -STEPS + (g + 1) * NB * T + .11), "stack", g))
        for n in range(NT):
            p.append((-T + n // SEQ + 1.55 + .05 * (n % SEQ), "v", n))
        for u in range(U):
            p += [((u - 1) * T - AHEAD + m // MPS + .2 * (m % MPS), "max", u * MT + m) for m in range(MT)]
            p.append((u * T - AHEAD + .25, "neg", u))
            end = (u + 1) * T
            p.append((end + .75, "raw", u))
            p += [(end + 1.45 + n, "norm", u * NP + n) for n in range(NP)]
            p.append((end + (3.4 if T >= 4 else 1.9), "attn", u))
        for s in range(STEPS):
            p += [(s + .1, "score", 2 * s), (s + .3, "score", 2 * s + 1), (s + 1.5, "value", s)]
        out_at = STEPS + (4.2 if T >= 4 else 2)
        gap = .9 if last_level else .4 if T == 1 else .8
        if below:
            p.append((out_at - 2, "coarse", 0) if not last_level else (0, "nothing", 0))
        if last_level:
            p += [(out_at + gap * (n - 2) + .05, "fetch", n) for n in range(OT)]
        p += [(out_at + gap * n, "out", n) for n in range(OT)]
        if not last_level:
            p.append((out_at + gap * OT, "interp", 0))
        return sorted(q for q in p if q[1] != "nothing")

    line, cut, LOOK = timeline(), CUT[lvl], 1 if last_level else 2
    assert line[-1][0] < cut + STEPS and line[0][0] >= cut - LOOK * STEPS, (line[0], line[-1])

    def window(lo, hi, offsets):
        p = sorted((k * STEPS + at, kind, n, k) for k in offsets for at, kind, n in line if lo <= k * STEPS + at < hi)
        return [(kind, k, n) for at, kind, n, k in p]

    ever = 100 * STEPS
    before = window(-ever, cut + STEPS, range(1, LOOK + 1))
    body = window(cut, cut + STEPS, range(LOOK + 1))
    end = window(cut, ever, range(LOOK))

    def bank_order(p, first):
        prev = {}
        for task in p:
            if task[0] in ("proj", "neg", "v", "out"):
                prev[task] = first
                first = task
        return prev, first and (first[0], first[1] - 1, first[2])

    prev_before, last_before = bank_order(before, None)
    prev_body, last_body = bank_order(body, last_before)
    assert last_before == last_body or N <= LOOK
    prev_end = bank_order(end, last_before)[0]

    with ExitStack() as ctx:
        def sb(name, shape, dt=F32):
            return ctx.enter_context(nc.sbuf_tensor(f"{name}{lvl}", shape, dt))

        def pb(name, shape):
            return ctx.enter_context(nc.psum_tensor(f"{name}{lvl}", shape, F32))

        signals = []

        def sig(name, per, step=1, lead=0):
            signals.append(Signal(ctx, nc, f"{name}_{lvl}", per, step, lead))
            return signals[-1]

        w_hi, w_lo = sb("w_hi", [128, WCOLS], F32R), sb("w_lo", [128, WCOLS], F32R)
        consts = sb("consts", [128, CCOLS])
        ident = sb("ident", [128, 128])
        x_in = sb("x_in", [128, XS, C])
        x_hi, x_lo = sb("x_hi", [128, 2, C], F32R), sb("x_lo", [128, 2, C], F32R)
        qk = sb("qk", [128, W])
        qk_bf = sb("qk_bf", [128, 2, 3, W], BF16)
        k_st = sb("k_st", [128, H, C], BF16)
        q_st = sb("q_st", [128, H, C], BF16)
        v_aug = sb("v_aug", [128, NT, H, 32])
        probs = sb("probs", [128, 2, HG, W])
        part_max = sb("part_max", [128, 2, NQ * HG, KB])
        row_max = sb("row_max", [128, 2, NQ, HG])
        neg_f = sb("neg_f", [HG, W])
        neg_bf = sb("neg_bf", [HG, 2, 2, W], BF16)
        raw = sb("raw", [128, W])
        attn = sb("attn", [128, 2, W])
        rec = sb("rec", [128, W // 32])
        a_hi, a_lo = sb("a_hi", [128, G, C], F32R), sb("a_lo", [128, G, C], F32R)
        bias_o = sb("bias_o", [128, 2])
        if last_level:
            up_ring_hi, up_ring_lo = sb("up_ring_hi", [128, 2, 2, 128], F32R), sb("up_ring_lo", [128, 2, 2, 128], F32R)
            xt_ring = sb("xt_ring", [128, 2, E])
            s_ring = sb("s_ring", [128, 4, E])
            bias_row = consts[:, CBOB:CBOB + E]
            stats = sb("stats", [128, 2, 6])
            moments = sb("moments", [128, 2, 2])
            var_eps = sb("var_eps", [128, 2])
            rstd = sb("rstd", [128, 2])
            minus_half = sb("minus_half", [128, 1])
        else:
            if below:
                c_hi, c_lo = sb("c_hi", [128, 2, C], F32R), sb("c_lo", [128, 2, C], F32R)
            cur, cur34 = sb("cur", [128, 2 * SEQ, S]), sb("cur34", [128, 2 * SEQ, S])
            fine = sb("fine", [128, 2 * SEQ, 2 * S])
            fine_hi, fine_lo = sb("fine_hi", [128, 2, 2 * C], F32R), sb("fine_lo", [128, 2, 2 * C], F32R)

        w_stage = probs[:, :, :, :].rearrange("p a h w -> p (a h w)")

        p_s = pb("p_s", [128, 4, 512])
        p_m = pb("p_m", [128, 2, 512])
        p_o = pb("p_o", [128, 512])
        p_a = pb("p_a", [128, 512])

        w_in_done = sig("w_in_done", 0, 16)
        w_hi_done, w_lo_done = sig("w_hi_done", 0), sig("w_lo_done", 0)
        const_done, set_done = sig("const_done", 0), sig("set_done", 0)
        x_loaded = [sig(f"x_loaded{c}", 1, 16) for c in range(2)]
        x_hi_done, x_lo_done = sig("x_hi_done", 2), sig("x_lo_done", 2)
        qk_mm, qk_read = sig("qk_mm", PT), sig("qk_read", PT)
        qk_rest_done, qk_b, qk_c = sig("qk_rest_done", PT), sig("qk_b", PT), sig("qk_c", PT)
        stored = [sig(f"stored{i}", PT // 2, 16) for i in range(2)]
        stacked = [sig(f"stacked{g}", 2 * len(K_PIECES), 16) for g in range(G)]
        v_mm, v_done = sig("v_mm", NT), sig("v_done", NT)
        max_mm, max_read, max_done = sig("max_mm", U * MT), sig("max_read", U * MT), sig("max_done", U)
        neg_mm, neg_read, neg_b = sig("neg_mm", U), sig("neg_read", U), sig("neg_b", U)
        neg_placed = [sig(f"neg_placed{i}", U // 2, 32) for i in range(2)]
        score_mm, exp_done = sig("score_mm", 2 * STEPS), sig("exp_done", 2 * STEPS)
        value_mm, raw_done = sig("value_mm", STEPS), sig("raw_done", U)
        turned_done, rec_done, spread_done = sig("turned_done", U * NP), sig("rec_done", U * NP), sig("spread_done", U * NP)
        attn_done = sig("attn_done", U)
        a_hi_done, a_lo_done = sig("a_hi_done", U), sig("a_lo_done", U, lead=1)
        out_mm, out_read = sig("out_mm", OT, lead=2), sig("out_read", OT, lead=2)
        if last_level:
            up_loaded = [sig(f"up_loaded{i}", OT // 2, 32) for i in range(2)]
            xt_loaded = [sig(f"xt_loaded{i}", OT // 2, 16) for i in range(2)]
            xt_biased = sig("xt_biased", OT, lead=2)
            stats_done, moments_done = sig("stats_done", OT), sig("moments_done", OT)
            eps_done, rstd_done = sig("eps_done", OT), sig("rstd_done", OT)
            y_done = sig("y_done", OT)
            y_stored = [sig(f"y_stored{i}", OT // 4, 16, lead=1) for i in range(4)]
        else:
            c_loaded = sig("c_loaded", 1, 32)
            cur34_done, fine_done = sig("cur34_done", 1), sig("fine_done", 1, lead=1)
            fine_hi_done, fine_lo_done = sig("fine_hi_done", 1), sig("fine_lo_done", 1, lead=1)
            fine_stored = sig("fine_stored", 1, 32, lead=1)
        held = sig("held", 0)

        def iterations(engine, steps):
            steps(before, lambda k: k - 1, prev_before)
            if N > LOOK:
                with engine.Fori(0, N - LOOK) as i:
                    steps(body, lambda k: (i, k), prev_body)
            steps(end, lambda k: N - LOOK + k, prev_end)

        def interleaved(scratch, it):
            return scratch.rearrange("p c (i t) -> i p c t", t=C)[number(it), :, :, :]

        with nc.Block() as block:
            @block.sync
            def _(sp):
                def hold():
                    sp.sem_inc(held.sem, 1)

                sp.dma_start(w_stage[:, 0:WCOLS], wpack[lvl, :, :]).then_inc(w_in_done.sem, 16)
                sp.dma_start(consts[:, :], cpack[lvl, :, :]).then_inc(w_in_done.sem, 16)
                sp.dma_start(ident[:, :], ident_in).then_inc(w_in_done.sem, 16)
                for s in y_stored if last_level else (fine_stored,):
                    s.open(sp)

                def store_y(it, n):
                    y_done.wait(sp, it, n + 1)
                    hold()
                    sp.dma_start(x1[number(it), n * 128:(n + 1) * 128, :], s_ring[:, n % 4, :])\
                      .then_inc(y_stored[n % 4].sem, 16)

                def steps(tasks, iteration, prev):
                    for kind, k, n in tasks:
                        it = iteration(k)
                        if kind == "x":
                            for c in range(2):
                                x_lo_done.wait(sp, it, c - XS + 1)
                                hold()
                                rows = xt.rearrange("(i s) e t -> i s e t", s=SEQ)[number(it), :, c * 128:(c + 1) * 128, 0:S]
                                sp.dma_start(x_in[:, c % XS, :].rearrange("p (s t) -> p s t", s=SEQ), rows.rearrange("s p t -> p s t"))\
                                  .then_inc(x_loaded[c].sem, 16)
                        elif kind == "coarse":
                            out_mm.wait(sp, it, 0)
                            hold()
                            sp.dma_start(c_hi[:, :, :].bitcast(F32), interleaved(up_hi[lvl], it)).then_inc(c_loaded.sem, 16)
                            sp.dma_start(c_lo[:, :, :].bitcast(F32), interleaved(up_lo[lvl], it)).then_inc(c_loaded.sem, 16)
                        elif kind == "proj":
                            t, m, blk = proj(n)
                            qk_c.wait(sp, it, n + 1)
                            hold()
                            for g in (2 * m, 2 * m + 1):
                                stacked[g].wait(sp, it, 0)
                                hold()
                            sp.dma_start(scr[t, :, m * 128:(m + 1) * 128, blk * W:(blk + 1) * W].rearrange("i p t -> p i t"),
                                         qk_bf[:, n % 2, :, :]).then_inc(stored[n % 2].sem, 16)
                        elif kind == "stack":
                            for i in range(2):
                                stored[i].wait(sp, it, (n // 2 + 1) * NB)
                                hold()
                            score_mm.wait(sp, earlier(it), 2 * (n + 1) * NB * T)
                            hold()
                            for r in range(len(K_PIECES)):
                                for t, st, pieces in ((0, q_st, Q_PIECES), (1, k_st, K_PIECES)):
                                    sp.dma_start(st[16 * r:16 * r + 16, HG * n:HG * n + HG, :],
                                                 scr[t, pieces[r], n * 64:(n + 1) * 64, 0:C].rearrange("(h d) t -> d h t", d=16))\
                                      .then_inc(stacked[n].sem, 16)
                        elif kind == "neg":
                            g, blk = unit(n)
                            neg_b.wait(sp, it, n + 1)
                            hold()
                            for i in range(2):
                                sp.dma_start(q_st[ROWS + i:ROWS + i + 1, HG * g:HG * g + HG, blk * W:(blk + 1) * W],
                                             neg_bf[0:HG, n % 2, i, :]).then_inc(neg_placed[n % 2].sem, 16)
                        elif kind == "fetch":
                            out_mm.wait(sp, it, n - 1)
                            hold()
                            for src, dst in ((up_hi, up_ring_hi), (up_lo, up_ring_lo)):
                                sp.dma_start(dst[:, n % 2, :, :].bitcast(F32), interleaved(src[0], it)[:, :, n * 128:(n + 1) * 128])\
                                  .then_inc(up_loaded[n % 2].sem, 16)
                            xt_biased.wait(sp, it, n - 1)
                            hold()
                            sp.dma_start(xt_ring[:, n % 2, :], xtok[number(it), n * 128:(n + 1) * 128, :])\
                              .then_inc(xt_loaded[n % 2].sem, 16)
                        elif kind == "out" and last_level:
                            if n >= 2:
                                store_y(it, n - 2)
                            if n == OT - 1:
                                store_y(it, n - 1)
                                store_y(it, n)
                        elif kind == "interp":
                            fine_hi_done.wait(sp, it, 1)
                            hold()
                            dst_hi, dst_lo = [u[lvl - 1].rearrange("p c (i t) -> i p c t", t=2 * C)[number(it), :, :, :]
                                              for u in (up_hi, up_lo)]
                            sp.dma_start(dst_hi, fine_hi[:, :, :].bitcast(F32)).then_inc(fine_stored.sem, 16)
                            fine_lo_done.wait(sp, it, 1)
                            hold()
                            sp.dma_start(dst_lo, fine_lo[:, :, :].bitcast(F32)).then_inc(fine_stored.sem, 16)

                iterations(sp, steps)
                if last_level:
                    for s in y_stored:
                        s.wait(sp, N - 1, OT // 4)
                else:
                    fine_stored.wait(sp, N - 1, 1)
                for s in stored:
                    s.wait(sp, N - 1, PT // 2)

            @block.gpsimd
            def _(pool):
                pool.memset(v_aug[:, :, :, HD + 1:32], 0.0).then_inc(set_done.sem, 1)
                pool.wait_ge(set_done.sem, 1)
                pool.memset(v_aug[:, :, :, HD:HD + 1], 1.0).then_inc(set_done.sem, 1)
                pool.wait_ge(set_done.sem, 2)
                pool.memset(k_st[ROWS:ROWS + 2, :, :], 1.0).then_inc(set_done.sem, 1)
                pool.wait_ge(set_done.sem, 3)
                a_lo_done.open(pool)
                if last_level:
                    pool.memset(minus_half[:, :], -0.5).then_inc(set_done.sem, 1)
                    pool.wait_ge(set_done.sem, 4)
                else:
                    fine_lo_done.open(pool)

                def steps(tasks, iteration, prev):
                    for kind, k, n in tasks:
                        it = iteration(k)
                        if kind == "x":
                            for c in range(2):
                                x_hi_done.wait(pool, it, c + 1)
                                v_mm.wait(pool, it, 0)
                                pool.tensor_tensor(out=x_lo[:, c, :], in0=x_in[:, c % XS, :], in1=x_hi[:, c, :], op=ALU.subtract)\
                                    .then_inc(x_lo_done.sem, 1)
                        elif kind == "proj":
                            bf = qk_bf[:, n % 2, :, :]
                            qk_read.wait(pool, it, n + 1)
                            pool.tensor_tensor(out=qk[:, :], in0=qk[:, :], in1=bf[:, 0, :], op=ALU.subtract)\
                                .then_inc(qk_rest_done.sem, 1)
                            qk_rest_done.wait(pool, it, n + 1)
                            pool.sem_inc(held.sem, 1)
                            pool.tensor_copy(bf[:, 1, :], qk[:, :]).then_inc(qk_b.sem, 1)
                            qk_b.wait(pool, it, n + 1)
                            pool.tensor_tensor(out=bf[:, 2, :], in0=qk[:, :], in1=bf[:, 1, :], op=ALU.subtract)\
                                .then_inc(qk_c.sem, 1)
                        elif kind == "neg":
                            neg_read.wait(pool, it, n + 1)
                            pool.tensor_tensor(out=neg_bf[:, n % 2, 1, :], in0=neg_f[:, :],
                                               in1=neg_bf[:, n % 2, 0, :], op=ALU.subtract).then_inc(neg_b.sem, 1)
                        elif kind == "norm" and n % NP == NP - 1:
                            u = n // NP
                            spread_done.wait(pool, it, n + 1)
                            pool.tensor_tensor(out=attn[:, u % 2, :], in0=raw[:, :], in1=attn[:, u % 2, :], op=ALU.mult)\
                                .then_inc(attn_done.sem, 1)
                        elif kind == "attn":
                            g, blk = unit(n)
                            a_hi_done.wait(pool, it, n + 1)
                            pool.tensor_tensor(out=a_lo[:, g, blk * W:(blk + 1) * W], in0=attn[:, n % 2, :],
                                               in1=a_hi[:, g, blk * W:(blk + 1) * W], op=ALU.subtract)\
                                .then_inc(a_lo_done.sem, 1)
                        elif kind == "out" and last_level:
                            eps_done.wait(pool, it, n + 1)
                            pool.tensor_tensor(out=rstd[:, n % 2:n % 2 + 1], in0=var_eps[:, n % 2:n % 2 + 1],
                                               in1=minus_half[:, :], op=ALU.pow).then_inc(rstd_done.sem, 1)
                        elif kind == "interp":
                            fine_hi_done.wait(pool, it, 1)
                            fine_stored.wait(pool, it, 0)
                            pool.tensor_tensor(out=fine_lo[:, :, :], in0=fine[:, :, :].rearrange("p (c s) t -> p c (s t)", c=2),
                                               in1=fine_hi[:, :, :], op=ALU.subtract).then_inc(fine_lo_done.sem, 1)

                iterations(pool, steps)

            @block.scalar
            def _(act):
                act.wait_ge(w_in_done.sem, 48)
                act.activation(w_hi[:, :], w_stage[:, 0:WCOLS], ACT.Copy).then_inc(w_hi_done.sem, 1)
                if not last_level:
                    out_read.open(act)

                def steps(tasks, iteration, prev):
                    for kind, k, n in tasks:
                        it = iteration(k)
                        if kind == "x":
                            for c in range(2):
                                x_loaded[c].wait(act, it, 1)
                                v_mm.wait(act, it, 0)
                                act.activation(x_hi[:, c, :], x_in[:, c % XS, :], ACT.Copy).then_inc(x_hi_done.sem, 1)
                        elif kind == "proj":
                            t, m, blk = proj(n)
                            col = CBQK + 2 * t + m
                            qk_mm.wait(act, it, n + 1)
                            qk_c.wait(act, it, n)
                            stored[n % 2].wait(act, it, n // 2)
                            act.activation(qk[:, :], p_a[:, 0:W], ACT.Identity, bias=consts[:, col:col + 1])
                            act.activation(qk_bf[:, n % 2, 0, :], p_a[:, 0:W], ACT.Identity, bias=consts[:, col:col + 1])\
                               .then_inc(qk_read.sem, 1)
                        elif kind == "neg":
                            neg_mm.wait(act, it, n + 1)
                            neg_b.wait(act, it, n)
                            neg_placed[n % 2].wait(act, it, n // 2)
                            act.activation(neg_f[:, :], p_a[0:HG, 0:W], ACT.Copy, scale=-1.0)
                            act.activation(neg_bf[:, n % 2, 0, :], p_a[0:HG, 0:W], ACT.Copy, scale=-1.0).then_inc(neg_read.sem, 1)
                        elif kind == "score":
                            s, p = divmod(n, 2)
                            score_mm.wait(act, it, n + 1)
                            value_mm.wait(act, it, s - 1)
                            act.activation(probs[:, s % 2, 2 * p:2 * p + 2, :], p_s[:, 2 * p:2 * p + 2, 0:W], ACT.Exp,
                                           scale=HD ** -0.5).then_inc(exp_done.sem, 1)
                        elif kind == "raw":
                            value_mm.wait(act, it, (n + 1) * T)
                            attn_done.wait(act, it, n)
                            act.activation(raw[:, :], p_o[:, 0:W], ACT.Copy).then_inc(raw_done.sem, 1)
                        elif kind == "attn":
                            g, blk = unit(n)
                            attn_done.wait(act, it, n + 1)
                            if g == 0:
                                out_mm.wait(act, earlier(it), (blk + 1) * OT // NB)
                            act.activation(a_hi[:, g, blk * W:(blk + 1) * W], attn[:, n % 2, :], ACT.Copy)\
                               .then_inc(a_hi_done.sem, 1)
                        elif kind == "out" and not last_level:
                            out_mm.wait(act, it, n + 1)
                            fine_done.wait(act, it, 0)
                            act.activation(cur[:, n * SEQ:(n + 1) * SEQ, :].rearrange("p s t -> p (s t)"), p_a[:, 0:W], ACT.Identity,
                                           bias=bias_o[:, n:n + 1]).then_inc(out_read.sem, 1)
                        elif kind == "interp":
                            fine_done.wait(act, it, 1)
                            fine_stored.wait(act, it, 0)
                            act.activation(fine_hi[:, :, :], fine[:, :, :].rearrange("p (c s) t -> p c (s t)", c=2), ACT.Copy)\
                               .then_inc(fine_hi_done.sem, 1)

                act.wait_ge(const_done.sem, 1)
                iterations(act, steps)

            @block.vector
            def _(dve):
                dve.wait_ge(w_in_done.sem, 48)
                dve.wait_ge(w_hi_done.sem, 1)
                dve.tensor_tensor(out=w_lo[:, :], in0=w_stage[:, 0:WCOLS], in1=w_hi[:, :], op=ALU.subtract)\
                   .then_inc(w_lo_done.sem, 1)
                if last_level:
                    dve.tensor_tensor(out=bias_row, in0=consts[:, CBOB:CBOB + E], in1=consts[:, CBUPB:CBUPB + E],
                                      op=ALU.add).then_inc(const_done.sem, 1)
                    xt_biased.open(dve)
                    out_read.open(dve)
                else:
                    dve.tensor_tensor(out=bias_o[:, :], in0=consts[:, CBO:CBO + 2], in1=consts[:, CBUP:CBUP + 2],
                                      op=ALU.add).then_inc(const_done.sem, 1)
                    fine_done.open(dve)
                dve.wait_ge(const_done.sem, 1)

                def finish_y(it, n):
                    rstd_done.wait(dve, it, n + 1)
                    dve.tensor_scalar(s_ring[:, n % 4, :], s_ring[:, n % 4, :], moments[:, n % 2, 0:1],
                                      rstd[:, n % 2:n % 2 + 1], ALU.subtract, ALU.mult).then_inc(y_done.sem, 1)

                def steps(tasks, iteration, prev):
                    for kind, k, n in tasks:
                        it = iteration(k)
                        if kind == "max":
                            u, m = divmod(n, MT)
                            max_mm.wait(dve, it, n + 1)
                            if m == 0:
                                neg_mm.wait(dve, it, u - 1)
                            slot = row_max[:, u % 2, :, :].rearrange("p q h -> p (q h)")
                            if KB > 1:
                                out = part_max[:, u % 2, m // KB, m % KB:m % KB + 1]
                            else:
                                out = slot[:, m * QP:(m + 1) * QP]
                            src = p_m[:, m % 2, :].rearrange("p (r t) -> p r t", r=QP) if QP > 1 else p_m[:, m % 2, :]
                            dve.reduce_max(out, src, AX.X).then_inc(max_read.sem, 1)
                            if KB > 1 and m == MT - 1:
                                max_read.wait(dve, it, n + 1)
                                dve.tensor_tensor(out=slot, in0=part_max[:, u % 2, :, 0], in1=part_max[:, u % 2, :, 1], op=ALU.max)\
                                   .then_inc(max_done.sem, 1)
                        elif kind == "v":
                            v_mm.wait(dve, it, n + 1)
                            value_mm.wait(dve, earlier(it), STEPS - T + n // SEQ + 1)
                            dve.tensor_tensor(out=v_aug[:, n, :, 0:HD], in0=p_a[:, 0:E].rearrange("p (h d) -> p h d", d=HD),
                                              in1=consts[:, CBV:CBV + E].rearrange("p (h d) -> p h d", d=HD), op=ALU.add)\
                               .then_inc(v_done.sem, 1)
                        elif kind == "norm":
                            u, part = divmod(n, NP)
                            cols = slice(part * W // NP, (part + 1) * W // NP)
                            if part == 0:
                                raw_done.wait(dve, it, u + 1)
                                a_lo_done.wait(dve, it, u - 1)
                                dve.sem_inc(held.sem, 1)
                            out, inv = attn[:, u % 2, cols], rec[:, part * W // NP // 32:(part + 1) * W // NP // 32]
                            dve.transpose(out, raw[:, cols]).then_inc(turned_done.sem, 1)
                            turned_done.wait(dve, it, n + 1)
                            dve.reciprocal(inv, out.rearrange("p (c r) -> p c r", r=32)[:, :, HD]).then_inc(rec_done.sem, 1)
                            rec_done.wait(dve, it, n + 1)
                            dve.transpose(out, inv.unsqueeze(2).broadcast_to((128, W // NP // 32, 32))).then_inc(spread_done.sem, 1)
                        elif kind == "out" and last_level:
                            xt_loaded[n % 2].wait(dve, it, n // 2 + 1)
                            y_stored[n % 4].wait(dve, it, n // 4)
                            dve.tensor_tensor(out=s_ring[:, n % 4, :], in0=xt_ring[:, n % 2, :], in1=bias_row, op=ALU.add)\
                               .then_inc(xt_biased.sem, 1)
                            out_mm.wait(dve, it, n + 1)
                            xt_biased.wait(dve, it, n + 1)
                            dve.tensor_tensor(out=s_ring[:, n % 4, :], in0=p_a[:, 0:E], in1=s_ring[:, n % 4, :], op=ALU.add)\
                               .then_inc(out_read.sem, 1)
                            out_read.wait(dve, it, n + 1)
                            dve.bn_stats(stats[:, n % 2, :], s_ring[:, n % 4, :]).then_inc(stats_done.sem, 1)
                            stats_done.wait(dve, it, n + 1)
                            dve.sem_inc(held.sem, 1)
                            dve.bn_aggr(moments[:, n % 2, :], stats[:, n % 2, :]).then_inc(moments_done.sem, 1)
                            moments_done.wait(dve, it, n + 1)
                            dve.tensor_scalar(var_eps[:, n % 2:n % 2 + 1], moments[:, n % 2, 1:2], EPS, None, ALU.add)\
                               .then_inc(eps_done.sem, 1)
                            if n > 0:
                                finish_y(it, n - 1)
                            if n == OT - 1:
                                finish_y(it, n)
                        elif kind == "interp":
                            out_read.wait(dve, it, OT)
                            fine_lo_done.wait(dve, it, 0)
                            dve.tensor_scalar(cur34[:, :, :], cur[:, :, :], 0.75, None, ALU.mult).then_inc(cur34_done.sem, 1)
                            cur34_done.wait(dve, it, 1)
                            runs = [(0, r) for r in shifted(S, -1)] + [(S, r) for r in shifted(S, 1)]
                            for at, (dst, src, size) in runs:
                                ins = dve.scalar_tensor_tensor(out=fine[:, :, at + dst:at + dst + size], in0=cur[:, :, src:src + size],
                                                               scalar=0.25, in1=cur34[:, :, dst:dst + size],
                                                               op0=ALU.mult, op1=ALU.add)
                            ins.then_inc(fine_done.sem, 1)

                iterations(dve, steps)

            @block.tensor
            def _(pe):
                pe.wait_ge(w_hi_done.sem, 1)
                pe.wait_ge(w_lo_done.sem, 1)
                pe.wait_ge(set_done.sem, 3)
                out_mm.open(pe)

                def three(out, pairs):
                    terms = [t for (a_h, a_l), (b_h, b_l) in pairs for t in ((a_h, b_h), (a_l, b_h), (a_h, b_l))]
                    for n, (a, c) in enumerate(terms):
                        ins = pe.matmul(out, a, c, start=n == 0, stop=n == len(terms) - 1)
                    return ins

                def steps(tasks, iteration, prev):
                    for task in tasks:
                        kind, k, n = task
                        it = iteration(k)
                        if task in prev and prev[task]:
                            was, at, m = prev[task]
                            {"proj": qk_read, "neg": neg_read, "v": v_done, "out": out_read}[was].wait(pe, iteration(at), m + 1)
                        if kind == "proj":
                            t, m, blk = proj(n)
                            if n == 0:
                                x_hi_done.wait(pe, it, 2)
                                x_lo_done.wait(pe, it, 2)
                            cols = [slice(WQK + c * 512 + t * 256 + m * 128, WQK + c * 512 + t * 256 + m * 128 + 128) for c in range(2)]
                            tok = slice(blk * W, (blk + 1) * W)
                            three(p_a[:, 0:W], [((w_hi[:, cols[c]], w_lo[:, cols[c]]), (x_hi[:, c, tok], x_lo[:, c, tok]))
                                                for c in range(2)]).then_inc(qk_mm.sem, 1)
                        elif kind == "neg":
                            if KB > 1:
                                max_done.wait(pe, it, n + 1)
                            else:
                                max_read.wait(pe, it, (n + 1) * MT)
                            for q in range(NQ):
                                ins = pe.transpose(p_a[0:HG, q * 128:(q + 1) * 128], row_max[:, n % 2, q, :], ident[:, :])
                            ins.then_inc(neg_mm.sem, 1)
                        elif kind == "v":
                            at = (n % SEQ) * S + (n // SEQ) * 128
                            tok = slice(at, at + 128)
                            wc = [slice(WV + c * 256, WV + (c + 1) * 256) for c in range(2)]
                            three(p_a[:, 0:E], [((x_hi[:, c, tok], x_lo[:, c, tok]), (w_hi[:, wc[c]], w_lo[:, wc[c]]))
                                                for c in range(2)]).then_inc(v_mm.sem, 1)
                        elif kind == "out":
                            if n == 0:
                                a_lo_done.wait(pe, it, U)
                            if last_level:
                                tok = slice(n * 128, (n + 1) * 128)
                                up_loaded[n % 2].wait(pe, it, n // 2 + 1)
                                pairs = [((a_hi[:, g, tok], a_lo[:, g, tok]),
                                          (w_hi[:, WO + g * E:WO + (g + 1) * E], w_lo[:, WO + g * E:WO + (g + 1) * E])) for g in range(G)]
                                pairs += [((up_ring_hi[:, n % 2, c, :], up_ring_lo[:, n % 2, c, :]),
                                           (w_hi[:, WUP + c * E:WUP + (c + 1) * E], w_lo[:, WUP + c * E:WUP + (c + 1) * E])) for c in range(2)]
                                three(p_a[:, 0:E], pairs).then_inc(out_mm.sem, 1)
                            else:
                                def wcol(base, c):
                                    at = slice(base + c * E + n * 128, base + c * E + n * 128 + 128)
                                    return w_hi[:, at], w_lo[:, at]
                                pairs = [(wcol(WO, g), (a_hi[:, g, :], a_lo[:, g, :])) for g in range(G)]
                                if below:
                                    c_loaded.wait(pe, it, 1)
                                    pairs += [(wcol(WUP, c), (c_hi[:, c, :], c_lo[:, c, :])) for c in range(2)]
                                three(p_a[:, 0:W], pairs).then_inc(out_mm.sem, 1)
                        elif kind == "score":
                            s, p = divmod(n, 2)
                            u, kt = divmod(s, T)
                            g, blk = unit(u)
                            if kt == 0 and p == 0:
                                neg_placed[u % 2].wait(pe, it, u // 2 + 1)
                            exp_done.wait(pe, it, n - 1)
                            for j in (2 * p, 2 * p + 1):
                                for i in range(SEQ):
                                    key, at = i * S + kt * 128, blk * W + i * QS
                                    ins = pe.matmul(p_s[:, j, i * QS:(i + 1) * QS], k_st[0:ROWS + 2, HG * g + j, key:key + 128],
                                                    q_st[0:ROWS + 2, HG * g + j, at:at + QS], start=True, stop=True)
                            ins.then_inc(score_mm.sem, 1)
                        elif kind == "max":
                            u, m = divmod(n, MT)
                            g, blk = unit(u)
                            if m == 0:
                                stacked[g].wait(pe, it, 2 * len(K_PIECES))
                            max_read.wait(pe, it, n - 1)
                            for r in range(QP):
                                head, kb = divmod(m * QP + r, KB)
                                q, j = divmod(head, HG)
                                at = blk * W + q * 128
                                key = at // S * S + kb * QS
                                ins = pe.matmul(p_m[:, m % 2, r * QS:(r + 1) * QS], q_st[0:ROWS, HG * g + j, at:at + 128],
                                                k_st[0:ROWS, HG * g + j, key:key + QS], start=True, stop=True)
                            ins.then_inc(max_mm.sem, 1)
                        elif kind == "value":
                            u, kt = divmod(n, T)
                            g, blk = unit(u)
                            exp_done.wait(pe, it, 2 * n + 2)
                            if u == 0:
                                v_done.wait(pe, it, (kt + 1) * SEQ)
                            if kt == 0:
                                raw_done.wait(pe, it, u)
                            for i in range(SEQ):
                                cols = slice(i * QS, (i + 1) * QS)
                                for j in range(HG):
                                    ins = pe.matmul(p_o[32 * j:32 * j + 32, cols], v_aug[:, kt * SEQ + i, HG * g + j, :],
                                                    probs[:, n % 2, j, cols], start=kt == 0 and (i == 0 or T == 1),
                                                    stop=kt == T - 1 and (i == SEQ - 1 or T == 1))
                            ins.then_inc(value_mm.sem, 1)

                iterations(pe, steps)

        clear_semaphores(nc, signals)


W1COLS, HCOLS = 512, 1024
USES = 24
W3AT = 8 * W1COLS + 16 * HCOLS
FCOLS = W3AT + 8 * E


def w_cols(v):
    return (v * W1COLS, W1COLS) if v < 8 else (8 * W1COLS + (v - 8) * HCOLS, HCOLS)


def ffn(nc, x1, wf, scales, s3row, ident_in, lo_scr, out):
    with ExitStack() as ctx:
        def sb(name, shape, dt=F32):
            return ctx.enter_context(nc.sbuf_tensor(f"f_{name}", shape, dt))

        signals = []

        def sig(name, per, step=1, lead=0):
            signals.append(Signal(ctx, nc, f"f_{name}", per, step, lead))
            return signals[-1]

        w_hi = sb("w_hi", [128, FCOLS], F32R)
        w3_lo = sb("w3_lo", [128, 8 * E], F32R)
        lo_ring = sb("lo_ring", [128, 3, HCOLS], F32R)
        xa = sb("xa", [128, 2, 4, E])
        xt_hi, xt_lo = sb("xt_hi", [128, 2, 512], F32R), sb("xt_lo", [128, 2, 512], F32R)
        h_hi, h_lo = sb("h_hi", [128, 2, 8, 512], F32R), sb("h_lo", [128, 2, 8, 512], F32R)
        gate = sb("gate", [128, 2, 512])
        h_f = sb("h_f", [128, 2, 512])
        sc = sb("sc", [128, 32])
        s3 = sb("s3", [128, E])
        ident = sb("ident", [128, 128])
        s_ring = sb("s_ring", [128, 2, E])
        stats, moments = sb("stats", [128, 2, 6]), sb("moments", [128, 2, 2])
        var_eps, rstd, minus_half = sb("var_eps", [128, 2]), sb("rstd", [128, 2]), sb("minus_half", [128, 1])
        p_h = ctx.enter_context(nc.psum_tensor("p_h", [128, 4, 512], F32))
        p_t = ctx.enter_context(nc.psum_tensor("p_t", [128, 2, 512], F32))
        p_y = ctx.enter_context(nc.psum_tensor("p_y", [128, 2, 512], F32))

        const_in, raw_in = sig("const_in", 0), [sig(f"raw_in{i}", 0) for i in range(2)]
        prep_hi, prep_lo = sig("prep_hi", 0), sig("prep_lo", 0)
        prep_stored = [sig(f"prep_stored{i}", 0) for i in range(3)]
        set_done = sig("set_done", 0)
        x_in = sig("x_in", 1, 16)
        t_mm, t_hi, t_lo = sig("t_mm", 2), sig("t_hi", 2), sig("t_lo", 2)
        lo_in = [sig(f"lo_in{i}", USES // 3, 16) for i in range(3)]
        h_mm = sig("h_mm", 32, lead=3)
        act_read = sig("act_read", 24, lead=4)
        gated = sig("gated", 8, lead=2)
        hi_done, lo_done = sig("hi_done", 24), sig("lo_done", 24, lead=2)
        y_mm, y_scaled, y_sum = sig("y_mm", 4, lead=1), sig("y_scaled", 4, lead=2), sig("y_sum", 4, lead=5)
        stats_done, moments_done = sig("stats_done", 4), sig("moments_done", 4)
        eps_done, rstd_done, y_done = sig("eps_done", 4), sig("rstd_done", 4), sig("y_done", 4)
        stored = [sig(f"stored{i}", 2, 16, lead=1) for i in range(2)]
        held = sig("held", 0)
        PREP = [w_cols(v) for v in range(USES)] + [(W3AT, HCOLS), (W3AT + HCOLS, HCOLS)]

        def bank(v, which=0):
            return 2 * v + which if v < 8 else 16 + v - 8

        def halves(engine, steps):
            with engine.Fori(0, B) as b:
                for half in range(2):
                    steps(b, half, (b * 2, half))

        with nc.Block() as block:
            @block.sync
            def _(sp):
                for dst, src in ((sc, scales), (s3, s3row), (ident, ident_in)):
                    sp.dma_start(dst[:, :], src).then_inc(const_in.sem, 16)
                def store_lo(engine, n):
                    engine.wait_ge(prep_lo.sem, n + 1)
                    col, k = PREP[n]
                    engine.dma_start(lo_scr[:, col:col + k], lo_ring[:, n % 3, 0:k].bitcast(F32)).then_inc(prep_stored[n % 3].sem, 16)

                for n, (col, k) in enumerate(PREP):
                    if n >= 2:
                        sp.wait_ge(prep_lo.sem, n - 1)
                    sp.dma_start(xa[:, n % 2, :, :].rearrange("p a e -> p (a e)")[:, 0:k], wf[:, col:col + k])\
                      .then_inc(raw_in[n % 2].sem, 16)
                    if 1 <= n <= USES:
                        store_lo(sp, n - 1)
                for i in range(3):
                    sp.wait_ge(prep_stored[i].sem, 16 * (USES // 3))
                sp.wait_ge(prep_lo.sem, len(PREP))

                def steps(b, half, hh):
                    y_sum.wait(sp, hh, -4)
                    sp.sem_inc(held.sem, 1)
                    sp.dma_start(xa[:, half, :, :], x1[b, half * 512:(half + 1) * 512, :].rearrange("(q p) e -> p q e", p=128))\
                      .then_inc(x_in.sem, 16)
                    for v in range(USES):
                        h_mm.wait(sp, hh, (bank(v - 3, 1 if v - 3 < 8 else 0) + 1) if v >= 3 else v - 2)
                        sp.sem_inc(held.sem, 1)
                        col, k = w_cols(v)
                        sp.dma_start(lo_ring[:, v % 3, 0:k].bitcast(F32), lo_scr[:, col:col + k]).then_inc(lo_in[v % 3].sem, 16)

                halves(sp, steps)

            @block.gpsimd
            def _(pool):
                pool.memset(minus_half[:, :], -0.5).then_inc(set_done.sem, 1)
                pool.wait_ge(set_done.sem, 1)
                def steps(b, half, hh):
                    for q in range(4):
                        eps_done.wait(pool, hh, q + 1)
                        pool.tensor_tensor(out=rstd[:, q % 2:q % 2 + 1], in0=var_eps[:, q % 2:q % 2 + 1],
                                           in1=minus_half[:, :], op=ALU.pow).then_inc(rstd_done.sem, 1)

                halves(pool, steps)

            @block.scalar
            def _(act):
                for n, (col, k) in enumerate(PREP):
                    act.wait_ge(raw_in[n % 2].sem, 16 * (n // 2 + 1))
                    act.activation(w_hi[:, col:col + k], xa[:, n % 2, :, :].rearrange("p a e -> p (a e)")[:, 0:k], ACT.Copy)\
                       .then_inc(prep_hi.sem, 1)
                act.wait_ge(const_in.sem, 48)
                act.sem_inc(act_read.sem, 4)
                for i in range(2):
                    act.sem_inc(stored[i].sem, 16)

                def steps(b, half, hh):
                    for c in range(2):
                        t_mm.wait(act, hh, c + 1)
                        act.activation(xt_hi[:, c, :], p_t[:, c, :], ACT.Copy).then_inc(t_hi.sem, 1)
                    for v in range(USES):
                        h_mm.wait(act, hh, bank(v) + 1)
                        if v < 8:
                            gated.wait(act, hh, v - 1)
                            act.activation(gate[:, v % 2, :], p_h[:, bank(v) % 4, :], ACT.Silu, scale=sc[:, v:v + 1])\
                               .then_inc(act_read.sem, 1)
                            gated.wait(act, hh, v + 1)
                        else:
                            lo_done.wait(act, hh, v - 1)
                            act.activation(h_f[:, v % 2, :], p_h[:, bank(v) % 4, :], ACT.Gelu, scale=sc[:, 8 + v:9 + v])\
                               .then_inc(act_read.sem, 1)
                            act_read.wait(act, hh, v + 1)
                        if v == 0:
                            y_mm.wait(act, hh, 0)
                        act.activation(h_hi[:, (v // 8) % 2, v % 8, :], h_f[:, v % 2, :], ACT.Copy).then_inc(hi_done.sem, 1)
                    for q in range(4):
                        y_done.wait(act, hh, q + 1)
                        row = half * 512 + q * 128
                        act.dma_start(out[b, row:row + 128, :], s_ring[:, q % 2, :]).then_inc(stored[q % 2].sem, 16)

                halves(act, steps)
                for i in range(2):
                    act.wait_ge(stored[i].sem, stored[i].at(2 * B - 1, 2))

            @block.vector
            def _(dve):
                for n, (col, k) in enumerate(PREP):
                    dve.wait_ge(prep_hi.sem, n + 1)
                    if n >= USES:
                        dst = w3_lo[:, (n - USES) * HCOLS:(n - USES + 1) * HCOLS]
                    else:
                        if n >= 3:
                            dve.wait_ge(prep_stored[n % 3].sem, 16 * (n // 3))
                        dst = lo_ring[:, n % 3, 0:k]
                    dve.tensor_tensor(out=dst, in0=xa[:, n % 2, :, :].rearrange("p a e -> p (a e)")[:, 0:k],
                                      in1=w_hi[:, col:col + k], op=ALU.subtract).then_inc(prep_lo.sem, 1)
                dve.wait_ge(const_in.sem, 48)
                for s, n in ((lo_done, 2), (y_scaled, 2), (y_sum, 5), (gated, 2)):
                    dve.sem_inc(s.sem, n)

                def finish(hh, q):
                    rstd_done.wait(dve, hh, q + 1)
                    dve.tensor_scalar(s_ring[:, q % 2, :], s_ring[:, q % 2, :], moments[:, q % 2, 0:1],
                                      rstd[:, q % 2:q % 2 + 1], ALU.subtract, ALU.mult).then_inc(y_done.sem, 1)

                def steps(b, half, hh):
                    for c in range(2):
                        t_hi.wait(dve, hh, c + 1)
                        dve.tensor_tensor(out=xt_lo[:, c, :], in0=p_t[:, c, :], in1=xt_hi[:, c, :], op=ALU.subtract)\
                           .then_inc(t_lo.sem, 1)
                    for v in range(USES):
                        if v < 8:
                            h_mm.wait(dve, hh, bank(v, 1) + 1)
                            act_read.wait(dve, hh, v + 1)
                            lo_done.wait(dve, hh, v - 1)
                            dve.scalar_tensor_tensor(out=h_f[:, v % 2, :], in0=p_h[:, bank(v, 1) % 4, :], scalar=sc[:, 8 + v:9 + v],
                                                     in1=gate[:, v % 2, :], op0=ALU.mult, op1=ALU.mult).then_inc(gated.sem, 1)
                        hi_done.wait(dve, hh, v + 1)
                        dve.tensor_tensor(out=h_lo[:, (v // 8) % 2, v % 8, :], in0=h_f[:, v % 2, :],
                                          in1=h_hi[:, (v // 8) % 2, v % 8, :], op=ALU.subtract).then_inc(lo_done.sem, 1)
                    for q in range(4):
                        y_mm.wait(dve, hh, q + 1)
                        stored[q % 2].wait(dve, hh, q // 2)
                        dve.tensor_tensor(out=s_ring[:, q % 2, :], in0=p_y[:, q % 2, 0:E], in1=s3[:, :], op=ALU.mult)\
                           .then_inc(y_scaled.sem, 1)
                        y_scaled.wait(dve, hh, q + 1)
                        dve.tensor_tensor(out=s_ring[:, q % 2, :], in0=s_ring[:, q % 2, :], in1=xa[:, half, q, :], op=ALU.add)\
                           .then_inc(y_sum.sem, 1)
                        y_sum.wait(dve, hh, q + 1)
                        dve.bn_stats(stats[:, q % 2, :], s_ring[:, q % 2, :]).then_inc(stats_done.sem, 1)
                        stats_done.wait(dve, hh, q + 1)
                        dve.sem_inc(held.sem, 1)
                        dve.bn_aggr(moments[:, q % 2, :], stats[:, q % 2, :]).then_inc(moments_done.sem, 1)
                        moments_done.wait(dve, hh, q + 1)
                        dve.tensor_scalar(var_eps[:, q % 2:q % 2 + 1], moments[:, q % 2, 1:2], EPS, None, ALU.add)\
                           .then_inc(eps_done.sem, 1)
                        if q > 0:
                            finish(hh, q - 1)
                    finish(hh, 3)

                halves(dve, steps)

            @block.tensor
            def _(pe):
                pe.wait_ge(prep_lo.sem, len(PREP))
                pe.wait_ge(const_in.sem, 48)
                pe.sem_inc(h_mm.sem, 3)
                pe.sem_inc(y_mm.sem, 1)

                def bank_free(hh, u):
                    p = u - 4
                    if 0 <= p < 16 and p % 2:
                        gated.wait(pe, hh, p // 2 + 1)
                    elif 0 <= p < 16:
                        act_read.wait(pe, hh, p // 2 + 1)
                    else:
                        act_read.wait(pe, hh, p + 1 if p < 0 else 8 + p - 16 + 1)

                def steps(b, half, hh):
                    x_in.wait(pe, hh, 1)
                    for c in range(2):
                        for q in range(4):
                            ins = pe.transpose(p_t[:, c, q * 128:(q + 1) * 128], xa[:, half, q, c * 128:(c + 1) * 128], ident[:, :])
                        ins.then_inc(t_mm.sem, 1)
                    t_lo.wait(pe, hh, 2)
                    for v in range(USES):
                        lo_in[v % 3].wait(pe, hh, v // 3 + 1)
                        col, _ = w_cols(v)
                        kinds = 2 if v < 8 else 1
                        chunks = 2 if v < 8 else 8
                        for which in range(kinds):
                            u = bank(v, which)
                            bank_free(hh, u)
                            for c in range(chunks):
                                at_c = (which * chunks + c) * 128
                                wh = w_hi[:, col + at_c:col + at_c + 128]
                                wl = lo_ring[:, v % 3, at_c:at_c + 128]
                                if v < 8:
                                    m_hi, m_lo = xt_hi[:, c, :], xt_lo[:, c, :]
                                else:
                                    src = (v // 8 - 1) % 2
                                    if v % 8 == 0:
                                        lo_done.wait(pe, hh, (v // 8 - 1) * 8 + c + 1)
                                    m_hi, m_lo = h_hi[:, src, c, :], h_lo[:, src, c, :]
                                o = p_h[:, u % 4, :]
                                pe.matmul(o, wh, m_hi, start=c == 0, stop=False)
                                pe.matmul(o, wl, m_hi, start=False, stop=False)
                                ins = pe.matmul(o, wh, m_lo, start=False, stop=c == chunks - 1)
                            ins.then_inc(h_mm.sem, 1)
                    for q in range(4):
                        tok = slice(q * 128, (q + 1) * 128)
                        y_scaled.wait(pe, hh, q - 1)
                        for c in range(8):
                            if q == 0:
                                lo_done.wait(pe, hh, 16 + c + 1)
                            o, at_c = p_y[:, q % 2, 0:E], c * E
                            wh, wl = w_hi[:, W3AT + at_c:W3AT + at_c + E], w3_lo[:, at_c:at_c + E]
                            pe.matmul(o, h_hi[:, 0, c, tok], wh, start=c == 0, stop=False)
                            pe.matmul(o, h_hi[:, 0, c, tok], wl, start=False, stop=False)
                            ins = pe.matmul(o, h_lo[:, 0, c, tok], wh, start=False, stop=c == 7)
                        ins.then_inc(y_mm.sem, 1)

                halves(pe, steps)


def program(nc, xt, xtok, wpack, cpack, wf, scales, s3row, ident, out):
    scr = nc.dram_tensor("qk_scratch", (2, 3, E, S0), BF16, kind="Internal").ap()
    up_hi = [nc.dram_tensor(f"up_hi{i}", (128, 2, B * (S0 >> i)), F32, kind="Internal").ap() for i in range(LEVELS - 1)]
    up_lo = [nc.dram_tensor(f"up_lo{i}", (128, 2, B * (S0 >> i)), F32, kind="Internal").ap() for i in range(LEVELS - 1)]
    x1 = nc.dram_tensor("x1", (B, S0, E), F32, kind="Internal").ap()
    lo_scr = nc.dram_tensor("w_lo_scratch", (128, FCOLS), F32, kind="Internal").ap()
    for lvl in reversed(range(LEVELS)):
        attention_level(nc, lvl, xt, xtok, wpack, cpack, ident, scr, up_hi, up_lo, x1)
    ffn(nc, x1, wf, scales, s3row, ident, lo_scr, out)


def kernel(**inputs):
    import concourse.bacc as bacc
    from concourse.bass_utils import run_bass_kernel_spmd as run

    a = {k: np.asarray(v) for k, v in inputs.items()}
    f = np.float32
    order = token_order()
    x = a["L0_attn_query"][:, order, :]
    iw, ib = a["L0_attn_in_proj_w"], a["L0_attn_in_proj_b"]

    def chunks(wt):
        return wt.reshape(-1, 128, wt.shape[1]).transpose(1, 0, 2).reshape(128, -1)

    wpack, cpack = np.zeros((LEVELS, 128, WCOLS), f), np.zeros((LEVELS, 128, CCOLS), f)
    for i in range(LEVELS):
        wpack[i, :, WQK:WV] = chunks(iw[i, :2 * E].T)
        wpack[i, :, WV:WO] = chunks(iw[i, 2 * E:].T)
        wo = np.zeros((H, 32, E), f)
        wo[:, :HD] = a["L0_attn_out_w"][i].T.reshape(H, HD, E)
        wpack[i, :, WO:WUP] = chunks(wo.reshape(H * 32, E))
        cpack[i, :, CBQK:CBO] = ib[i, :2 * E].reshape(4, 128).T
        cpack[i, :, CBO:CBUP] = a["L0_attn_out_b"][i].reshape(2, 128).T
        cpack[i, :, CBV:CBOB] = ib[i, 2 * E:]
        cpack[i, :, CBOB:CBUPB] = a["L0_attn_out_b"][i]
        if i < LEVELS - 1:
            wpack[i, :, WUP:] = chunks(a["L0_attn_up_w"][i].T)
            cpack[i, :, CBUP:CBV] = a["L0_attn_up_b"][i].reshape(2, 128).T
            cpack[i, :, CBUPB:] = a["L0_attn_up_b"][i]

    def tiles(*ws):
        return np.concatenate([chunks(w[m * 128:(m + 1) * 128].T) for m in range(8) for w in ws], axis=1)

    wf = np.concatenate([tiles(a["L0_ffn_w1_w"], a["L0_ffn_w2_w"]), tiles(a["L0_ffn_h1_w"]), tiles(a["L0_ffn_h2_w"]),
                         chunks(a["L0_ffn_w3_w"].T)], axis=1)
    scales = np.concatenate([a[f"L0_ffn_{n}_s"].reshape(8, 128).T for n in ("w1", "w2", "h1", "h2")], axis=1)
    arrays = {
        "xt": np.ascontiguousarray(x.transpose(0, 2, 1)), "xtok": np.ascontiguousarray(x), "wpack": wpack, "cpack": cpack,
        "wf": np.ascontiguousarray(wf), "scales": np.ascontiguousarray(scales),
        "s3row": np.ascontiguousarray(np.broadcast_to(a["L0_ffn_w3_s"], (128, E))), "ident": np.eye(128, dtype=f),
    }
    nc = bacc.Bacc("TRN2", target_bir_lowering=False, num_devices=1)
    args = [nc.dram_tensor(k, v.shape, mybir.dt.from_np(v.dtype), kind="ExternalInput").ap() for k, v in arrays.items()]
    args.append(nc.dram_tensor("y", (B, S0, E), F32, kind="ExternalOutput").ap())
    program(nc, *args)
    r = run(nc, [arrays], core_ids=[0])
    return r.results[0]["y"][:, np.argsort(order), :]
```

```python
import numpy as np
import concourse.bass as bass
from concourse import mybir
from contextlib import ExitStack

F32, F32R, BF16 = mybir.dt.float32, mybir.dt.float32r, mybir.dt.bfloat16
ALU, ACT, AX = mybir.AluOpType, mybir.ActivationFunctionType, mybir.AxisListType

B, S0, E = 8, 1024, 256
H, HD, LEVELS = 16, 16, 4
HG = 4
G = H // HG
DH = 1024
EPS = 1e-5
K_PIECES = (0, 0, 0, 1, 1, 2)
Q_PIECES = (0, 1, 2, 0, 1, 0)
ROWS = 16 * len(K_PIECES)
WQK, WV, WO, WUP = 0, 1024, 1536, 2560
WCOLS = 3072
CBQK, CBO, CBUP, CBV, CBOB, CBUPB = 0, 4, 6, 8, 264, 520
CCOLS = 776
NEG_AHEAD = (3, 3, 2, 1)
FRONT = ((-50.5, -44.5, 2.2), (-17.8, -15.5, 1.5), (-11.5, -9.8, 1.1), (-3.3, -2.8, .15))
V_AT = (None, (-9.9, .8), (-5.95, .3), (-2.2, .01))
CUT = (13.3, 9.3, 4.3, 3)


def token_order():
    order = np.arange(S0 >> (LEVELS - 1))
    for _ in range(LEVELS - 1):
        order = np.concatenate([2 * order, 2 * order + 1])
    return order


def shifted(n, by):
    order = np.arange(S0 >> (LEVELS - 1))
    while len(order) < n:
        order = np.concatenate([2 * order, 2 * order + 1])
    at = np.argsort(order)
    src = at[np.clip(order + by, 0, n - 1)]
    runs, i = [], 0
    while i < n:
        k = 1
        while i + k < n and src[i + k] == src[i] + k:
            k += 1
        runs.append((i, int(src[i]), k))
        i += k
    return runs


def clear_semaphores(nc, signals):
    with nc.Block() as block:
        @block.sync
        def _(sp):
            for s in signals:
                sp.sem_clear(s.sem)


class Signal:

    def __init__(self, ctx, nc, name, per, step=1, lead=0):
        self.sem, self.per, self.step, self.lead = ctx.enter_context(nc.semaphore(name)), per, step, lead

    def at(self, it, n):
        return it * (self.per * self.step) + (n + self.lead) * self.step

    def wait(self, engine, it, n):
        if isinstance(it, int):
            if self.at(it, n) > 0:
                engine.wait_ge(self.sem, self.at(it, n))
            return
        reg, k = it
        assert self.at(k, n) > 0, self.sem
        engine.wait_ge(self.sem, reg * (self.per * self.step) + self.at(k, n))

    def open(self, engine):
        engine.sem_inc(self.sem, self.lead * self.step)


def number(it):
    return it if isinstance(it, int) else it[0] + it[1]


def earlier(it):
    return it - 1 if isinstance(it, int) else (it[0], it[1] - 1)


def attention_level(nc, lvl, xt, xtok, wpack, cpack, ident_in, scr, up_hi, up_lo, x1):
    S = S0 >> lvl
    last_level = lvl == 0
    below = lvl < LEVELS - 1
    W = 512
    SEQ = max(1, W // S)
    N = B // SEQ
    C = SEQ * S
    T = S // 128
    NT = C // 128
    NB = C // W
    NQ = W // 128
    QS = min(S, W)
    QP = W // QS
    KB = S // QS
    U = G * NB
    STEPS = U * T
    MT = HG * NQ * KB // QP
    MPS = MT // T
    PT = 4 * NB
    OT = NT if last_level else 2
    NP = 2 if T >= 4 else 1
    XS = 1 if last_level else 2
    AHEAD = NEG_AHEAD[lvl]

    RUNS = [(src, dst, size, dst) for dst, src, size in shifted(S, -1)] + [(src, dst + S, size, dst) for dst, src, size in shifted(S, 1)]

    def proj(n):
        return (n // NB) % 2, n // (2 * NB), n % NB

    def unit(u):
        return u // NB, u % NB

    def timeline():
        p = []
        x_at, proj_at, proj_gap = FRONT[lvl]
        load_at = (x_at, x_at + (.3 if XS == 1 else .25) * (proj_at - x_at)) if T >= 4 else (x_at, x_at)
        cut_at = tuple(x_at + f * (proj_at - x_at) for f in ((.29, .7) if XS == 1 else (.6, .8)))
        p += [(load_at[c], "x", c) for c in range(2)] + [(cut_at[c], "cut", c) for c in range(2)]
        p += [(proj_at + proj_gap * n, "proj", n) for n in range(PT)]
        for g in range(G):
            p.append((max(proj_at + proj_gap * (2 * NB * (g // 2 + 1) - 1) + .01, -STEPS + (g + 1) * NB * T + .11), "stack", g))
        for n in range(NT):
            place = -T + n // SEQ + 1.55 + .05 * (n % SEQ)
            if last_level:
                p.append((place, "v", n))
            else:
                p += [(V_AT[lvl][0] + V_AT[lvl][1] * n, "v", n), (place, "place", n)]
        for u in range(U):
            p += [((u - 1) * T - AHEAD + m // MPS + .2 * (m % MPS), "max", u * MT + m) for m in range(MT)]
            p.append((u * T - AHEAD + .25, "neg", u))
            end = (u + 1) * T
            p.append((end + .75, "raw", u))
            p += [(end + 1.45 + n, "norm", u * NP + n) for n in range(NP)]
            p.append((end + (3.4 if T >= 4 else 1.9), "attn", u))
        for s in range(STEPS):
            p += [(s + .1, "score", 2 * s), (s + .3, "score", 2 * s + 1), (s + 1.5, "value", s)]
        out_at = STEPS + (4.2 if T >= 4 else 2)
        gap = .9 if last_level else .4 if T == 1 else .8
        if below and not last_level:
            p.append((out_at - 2, "coarse", 0))
        if last_level:
            p += [(out_at + gap * (n - 2) + .05, "fetch", n) for n in range(OT)]
        p += [(out_at + gap * n, "out", n) for n in range(OT)]
        if last_level:
            p += [(out_at + gap * n + .35, "stats", n) for n in range(OT)] + [(out_at + gap * n + .8, "finish", n) for n in range(OT)]
        else:
            blend_at, blend_gap = out_at + gap * OT, .3 if T == 4 else .1 if T == 2 else .02
            p += [(blend_at + blend_gap * n, "blend", n) for n in range(len(RUNS))]
            p.append((blend_at + blend_gap * len(RUNS), "interp", 0))
        return sorted(p)

    line, cut, LOOK = timeline(), CUT[lvl], 1 if last_level else 2
    assert line[-1][0] < cut + STEPS and line[0][0] >= cut - LOOK * STEPS, (line[0], line[-1])

    def window(lo, hi, offsets):
        p = sorted((k * STEPS + at, kind, n, k) for k in offsets for at, kind, n in line if lo <= k * STEPS + at < hi)
        return [(kind, k, n) for at, kind, n, k in p]

    ever = 100 * STEPS
    before = window(-ever, cut + STEPS, range(1, LOOK + 1))
    body = window(cut, cut + STEPS, range(LOOK + 1))
    end = window(cut, ever, range(LOOK))

    def bank_order(p, first):
        prev = {}
        for task in p:
            if task[0] in ("proj", "neg", "v", "out"):
                prev[task] = first
                first = task
        return prev, first and (first[0], first[1] - 1, first[2])

    prev_before, last_before = bank_order(before, None)
    prev_body, last_body = bank_order(body, last_before)
    assert last_before == last_body or N <= LOOK
    prev_end = bank_order(end, last_before)[0]

    with ExitStack() as ctx:
        def sb(name, shape, dt=F32):
            return ctx.enter_context(nc.sbuf_tensor(f"{name}{lvl}", shape, dt))

        def pb(name, shape):
            return ctx.enter_context(nc.psum_tensor(f"{name}{lvl}", shape, F32))

        signals = []

        def sig(name, per, step=1, lead=0):
            signals.append(Signal(ctx, nc, f"{name}_{lvl}", per, step, lead))
            return signals[-1]

        w_hi, w_lo = sb("w_hi", [128, WCOLS], F32R), sb("w_lo", [128, WCOLS], F32R)
        consts = sb("consts", [128, CCOLS])
        ident = sb("ident", [128, 128])
        x_in = sb("x_in", [128, XS, C])
        x_hi, x_lo = sb("x_hi", [128, 2, C], F32R), sb("x_lo", [128, 2, C], F32R)
        qk = sb("qk", [128, W])
        qk_bf = sb("qk_bf", [128, 2, 3, W], BF16)
        k_st = sb("k_st", [128, H, C], BF16)
        q_st = sb("q_st", [128, H, C], BF16)
        v_aug = sb("v_aug", [128, NT, H, 32])
        if not last_level:
            v_new = sb("v_new", [128, NT, E])
        probs = sb("probs", [128, 2, HG, W])
        part_max = sb("part_max", [128, 2, NQ * HG, KB])
        row_max = sb("row_max", [128, 2, NQ, HG])
        neg_f = sb("neg_f", [HG, W])
        neg_bf = sb("neg_bf", [HG, 2, 2, W], BF16)
        raw = sb("raw", [128, W])
        attn = sb("attn", [128, 2, W])
        rec = sb("rec", [128, W // 32])
        a_hi, a_lo = sb("a_hi", [128, G, C], F32R), sb("a_lo", [128, G, C], F32R)
        bias_o = sb("bias_o", [128, 2])
        if last_level:
            up_ring_hi, up_ring_lo = sb("up_ring_hi", [128, 2, 2, 128], F32R), sb("up_ring_lo", [128, 2, 2, 128], F32R)
            xt_ring = sb("xt_ring", [128, 2, E])
            s_ring = sb("s_ring", [128, 4, E])
            bias_row = consts[:, CBOB:CBOB + E]
            stats = sb("stats", [128, 2, 6])
            moments = sb("moments", [128, 2, 2])
            var_eps = sb("var_eps", [128, 2])
            rstd = sb("rstd", [128, 2])
            minus_half = sb("minus_half", [128, 1])
        else:
            if below:
                c_hi, c_lo = sb("c_hi", [128, 2, C], F32R), sb("c_lo", [128, 2, C], F32R)
            cur, cur34 = sb("cur", [128, 2 * SEQ, S]), sb("cur34", [128, 2 * SEQ, S])
            fine = sb("fine", [128, 2 * SEQ, 2 * S])
            fine_hi, fine_lo = sb("fine_hi", [128, 2, 2 * C], F32R), sb("fine_lo", [128, 2, 2 * C], F32R)

        w_stage = probs[:, :, :, :].rearrange("p a h w -> p (a h w)")

        p_s = pb("p_s", [128, 4, 512])
        p_m = pb("p_m", [128, 2, 512])
        p_o = pb("p_o", [128, 512])
        p_a = pb("p_a", [128, 512])

        w_in_done = sig("w_in_done", 0, 16)
        w_hi_done, w_lo_done = sig("w_hi_done", 0), sig("w_lo_done", 0)
        const_done, set_done = sig("const_done", 0), sig("set_done", 0)
        x_loaded = [sig(f"x_loaded{c}", 1, 16) for c in range(2)]
        x_hi_done, x_lo_done = sig("x_hi_done", 2), sig("x_lo_done", 2)
        qk_mm, qk_read = sig("qk_mm", PT), sig("qk_read", PT)
        qk_rest_done, qk_b, qk_c = sig("qk_rest_done", PT), sig("qk_b", PT), sig("qk_c", PT)
        stored = [sig(f"stored{i}", PT // 2, 16) for i in range(2)]
        stacked = [sig(f"stacked{g}", 2 * len(K_PIECES), 16) for g in range(G)]
        v_mm, v_done = sig("v_mm", NT), sig("v_done", NT)
        v_placed = v_done if last_level else sig("v_placed", NT)
        max_mm, max_read, max_done = sig("max_mm", U * MT), sig("max_read", U * MT), sig("max_done", U)
        neg_mm, neg_read, neg_b = sig("neg_mm", U), sig("neg_read", U), sig("neg_b", U)
        neg_placed = [sig(f"neg_placed{i}", U // 2, 32) for i in range(2)]
        score_mm, exp_done = sig("score_mm", 2 * STEPS), sig("exp_done", 2 * STEPS)
        value_mm, raw_done = sig("value_mm", STEPS), sig("raw_done", U)
        turned_done, rec_done, spread_done = sig("turned_done", U * NP), sig("rec_done", U * NP), sig("spread_done", U * NP)
        attn_done = sig("attn_done", U)
        a_hi_done, a_lo_done = sig("a_hi_done", U), sig("a_lo_done", U, lead=1)
        out_mm, out_read = sig("out_mm", OT, lead=2), sig("out_read", OT, lead=2)
        if last_level:
            up_loaded = [sig(f"up_loaded{i}", OT // 2, 32) for i in range(2)]
            xt_loaded = [sig(f"xt_loaded{i}", OT // 2, 16) for i in range(2)]
            xt_biased = sig("xt_biased", OT, lead=2)
            stats_done, moments_done = sig("stats_done", OT), sig("moments_done", OT)
            eps_done, rstd_done = sig("eps_done", OT), sig("rstd_done", OT)
            y_done = sig("y_done", OT)
            y_stored = [sig(f"y_stored{i}", OT // 4, 16, lead=1) for i in range(4)]
        else:
            c_loaded = sig("c_loaded", 1, 32)
            cur34_done, fine_done = sig("cur34_done", 1), sig("fine_done", len(RUNS), lead=1)
            fine_hi_done, fine_lo_done = sig("fine_hi_done", 1), sig("fine_lo_done", 1, lead=1)
            fine_stored = sig("fine_stored", 1, 32, lead=1)
        held = sig("held", 0)

        def iterations(engine, steps):
            steps(before, lambda k: k - 1, prev_before)
            if N > LOOK:
                with engine.Fori(0, N - LOOK) as i:
                    steps(body, lambda k: (i, k), prev_body)
            steps(end, lambda k: N - LOOK + k, prev_end)

        def interleaved(scratch, it):
            return scratch.rearrange("p c (i t) -> i p c t", t=C)[number(it), :, :, :]

        with nc.Block() as block:
            @block.sync
            def _(sp):
                def hold():
                    sp.sem_inc(held.sem, 1)

                sp.dma_start(w_stage[:, 0:WCOLS], wpack[lvl, :, :]).then_inc(w_in_done.sem, 16)
                sp.dma_start(consts[:, :], cpack[lvl, :, :]).then_inc(w_in_done.sem, 16)
                sp.dma_start(ident[:, :], ident_in).then_inc(w_in_done.sem, 16)
                for s in y_stored if last_level else (fine_stored,):
                    s.open(sp)

                def steps(tasks, iteration, prev):
                    for kind, k, n in tasks:
                        it = iteration(k)
                        if kind == "x":
                            x_lo_done.wait(sp, it, n - XS + 1)
                            hold()
                            rows = xt.rearrange("(i s) e t -> i s e t", s=SEQ)[number(it), :, n * 128:(n + 1) * 128, 0:S]
                            sp.dma_start(x_in[:, n % XS, :].rearrange("p (s t) -> p s t", s=SEQ), rows.rearrange("s p t -> p s t"))\
                              .then_inc(x_loaded[n].sem, 16)
                        elif kind == "coarse":
                            out_mm.wait(sp, it, 0)
                            hold()
                            sp.dma_start(c_hi[:, :, :].bitcast(F32), interleaved(up_hi[lvl], it)).then_inc(c_loaded.sem, 16)
                            sp.dma_start(c_lo[:, :, :].bitcast(F32), interleaved(up_lo[lvl], it)).then_inc(c_loaded.sem, 16)
                        elif kind == "proj":
                            t, m, blk = proj(n)
                            qk_c.wait(sp, it, n + 1)
                            hold()
                            for g in (2 * m, 2 * m + 1):
                                stacked[g].wait(sp, it, 0)
                                hold()
                            sp.dma_start(scr[t, :, m * 128:(m + 1) * 128, blk * W:(blk + 1) * W].rearrange("i p t -> p i t"),
                                         qk_bf[:, n % 2, :, :]).then_inc(stored[n % 2].sem, 16)
                        elif kind == "stack":
                            for i in range(2):
                                stored[i].wait(sp, it, (n // 2 + 1) * NB)
                                hold()
                            score_mm.wait(sp, earlier(it), 2 * (n + 1) * NB * T)
                            hold()
                            for r in range(len(K_PIECES)):
                                for t, st, pieces in ((0, q_st, Q_PIECES), (1, k_st, K_PIECES)):
                                    sp.dma_start(st[16 * r:16 * r + 16, HG * n:HG * n + HG, :],
                                                 scr[t, pieces[r], n * 64:(n + 1) * 64, 0:C].rearrange("(h d) t -> d h t", d=16))\
                                      .then_inc(stacked[n].sem, 16)
                        elif kind == "neg":
                            g, blk = unit(n)
                            neg_b.wait(sp, it, n + 1)
                            hold()
                            for i in range(2):
                                sp.dma_start(q_st[ROWS + i:ROWS + i + 1, HG * g:HG * g + HG, blk * W:(blk + 1) * W],
                                             neg_bf[0:HG, n % 2, i, :]).then_inc(neg_placed[n % 2].sem, 16)
                        elif kind == "fetch":
                            out_mm.wait(sp, it, n - 1)
                            hold()
                            for src, dst in ((up_hi, up_ring_hi), (up_lo, up_ring_lo)):
                                sp.dma_start(dst[:, n % 2, :, :].bitcast(F32), interleaved(src[0], it)[:, :, n * 128:(n + 1) * 128])\
                                  .then_inc(up_loaded[n % 2].sem, 16)
                            xt_biased.wait(sp, it, n - 1)
                            hold()
                            sp.dma_start(xt_ring[:, n % 2, :], xtok[number(it), n * 128:(n + 1) * 128, :])\
                              .then_inc(xt_loaded[n % 2].sem, 16)
                        elif kind == "finish":
                            y_done.wait(sp, it, n + 1)
                            hold()
                            sp.dma_start(x1[number(it), n * 128:(n + 1) * 128, :], s_ring[:, n % 4, :])\
                              .then_inc(y_stored[n % 4].sem, 16)
                        elif kind == "interp":
                            fine_hi_done.wait(sp, it, 1)
                            hold()
                            dst_hi, dst_lo = [u[lvl - 1].rearrange("p c (i t) -> i p c t", t=2 * C)[number(it), :, :, :]
                                              for u in (up_hi, up_lo)]
                            sp.dma_start(dst_hi, fine_hi[:, :, :].bitcast(F32)).then_inc(fine_stored.sem, 16)
                            fine_lo_done.wait(sp, it, 1)
                            hold()
                            sp.dma_start(dst_lo, fine_lo[:, :, :].bitcast(F32)).then_inc(fine_stored.sem, 16)

                iterations(sp, steps)
                if last_level:
                    for s in y_stored:
                        s.wait(sp, N - 1, OT // 4)
                else:
                    fine_stored.wait(sp, N - 1, 1)
                for s in stored:
                    s.wait(sp, N - 1, PT // 2)

            @block.gpsimd
            def _(pool):
                pool.memset(v_aug[:, :, :, HD + 1:32], 0.0).then_inc(set_done.sem, 1)
                pool.wait_ge(set_done.sem, 1)
                pool.memset(v_aug[:, :, :, HD:HD + 1], 1.0).then_inc(set_done.sem, 1)
                pool.wait_ge(set_done.sem, 2)
                pool.memset(k_st[ROWS:ROWS + 2, :, :], 1.0).then_inc(set_done.sem, 1)
                pool.wait_ge(set_done.sem, 3)
                a_lo_done.open(pool)
                if last_level:
                    pool.memset(minus_half[:, :], -0.5).then_inc(set_done.sem, 1)
                    pool.wait_ge(set_done.sem, 4)
                else:
                    fine_lo_done.open(pool)

                def steps(tasks, iteration, prev):
                    for kind, k, n in tasks:
                        it = iteration(k)
                        if kind == "cut":
                            x_hi_done.wait(pool, it, n + 1)
                            v_mm.wait(pool, it, 0)
                            pool.tensor_tensor(out=x_lo[:, n, :], in0=x_in[:, n % XS, :], in1=x_hi[:, n, :], op=ALU.subtract)\
                                .then_inc(x_lo_done.sem, 1)
                        elif kind == "proj":
                            bf = qk_bf[:, n % 2, :, :]
                            qk_read.wait(pool, it, n + 1)
                            pool.tensor_tensor(out=qk[:, :], in0=qk[:, :], in1=bf[:, 0, :], op=ALU.subtract)\
                                .then_inc(qk_rest_done.sem, 1)
                            qk_rest_done.wait(pool, it, n + 1)
                            pool.sem_inc(held.sem, 1)
                            pool.tensor_copy(bf[:, 1, :], qk[:, :]).then_inc(qk_b.sem, 1)
                            qk_b.wait(pool, it, n + 1)
                            pool.tensor_tensor(out=bf[:, 2, :], in0=qk[:, :], in1=bf[:, 1, :], op=ALU.subtract)\
                                .then_inc(qk_c.sem, 1)
                        elif kind == "place":
                            v_done.wait(pool, it, n + 1)
                            value_mm.wait(pool, earlier(it), STEPS - T + n // SEQ + 1)
                            pool.sem_inc(held.sem, 1)
                            pool.tensor_copy(v_aug[:, n, :, 0:HD], v_new[:, n, :].rearrange("p (h d) -> p h d", d=HD))\
                                .then_inc(v_placed.sem, 1)
                        elif kind == "neg":
                            neg_read.wait(pool, it, n + 1)
                            pool.tensor_tensor(out=neg_bf[:, n % 2, 1, :], in0=neg_f[:, :],
                                               in1=neg_bf[:, n % 2, 0, :], op=ALU.subtract).then_inc(neg_b.sem, 1)
                        elif kind == "norm" and n % NP == NP - 1:
                            u = n // NP
                            spread_done.wait(pool, it, n + 1)
                            pool.tensor_tensor(out=attn[:, u % 2, :], in0=raw[:, :], in1=attn[:, u % 2, :], op=ALU.mult)\
                                .then_inc(attn_done.sem, 1)
                        elif kind == "attn":
                            g, blk = unit(n)
                            a_hi_done.wait(pool, it, n + 1)
                            pool.tensor_tensor(out=a_lo[:, g, blk * W:(blk + 1) * W], in0=attn[:, n % 2, :],
                                               in1=a_hi[:, g, blk * W:(blk + 1) * W], op=ALU.subtract)\
                                .then_inc(a_lo_done.sem, 1)
                        elif kind == "stats":
                            eps_done.wait(pool, it, n + 1)
                            pool.tensor_tensor(out=rstd[:, n % 2:n % 2 + 1], in0=var_eps[:, n % 2:n % 2 + 1],
                                               in1=minus_half[:, :], op=ALU.pow).then_inc(rstd_done.sem, 1)
                        elif kind == "interp":
                            fine_hi_done.wait(pool, it, 1)
                            fine_stored.wait(pool, it, 0)
                            pool.tensor_tensor(out=fine_lo[:, :, :], in0=fine[:, :, :].rearrange("p (c s) t -> p c (s t)", c=2),
                                               in1=fine_hi[:, :, :], op=ALU.subtract).then_inc(fine_lo_done.sem, 1)

                iterations(pool, steps)

            @block.scalar
            def _(act):
                act.wait_ge(w_in_done.sem, 48)
                act.activation(w_hi[:, :], w_stage[:, 0:WCOLS], ACT.Copy).then_inc(w_hi_done.sem, 1)
                if not last_level:
                    out_read.open(act)

                def steps(tasks, iteration, prev):
                    for kind, k, n in tasks:
                        it = iteration(k)
                        if kind == "cut":
                            x_loaded[n].wait(act, it, 1)
                            v_mm.wait(act, it, 0)
                            act.activation(x_hi[:, n, :], x_in[:, n % XS, :], ACT.Copy).then_inc(x_hi_done.sem, 1)
                        elif kind == "proj":
                            t, m, blk = proj(n)
                            col = CBQK + 2 * t + m
                            qk_mm.wait(act, it, n + 1)
                            qk_c.wait(act, it, n)
                            stored[n % 2].wait(act, it, n // 2)
                            act.activation(qk[:, :], p_a[:, 0:W], ACT.Identity, bias=consts[:, col:col + 1])
                            act.activation(qk_bf[:, n % 2, 0, :], p_a[:, 0:W], ACT.Identity, bias=consts[:, col:col + 1])\
                               .then_inc(qk_read.sem, 1)
                        elif kind == "neg":
                            neg_mm.wait(act, it, n + 1)
                            neg_b.wait(act, it, n)
                            neg_placed[n % 2].wait(act, it, n // 2)
                            act.activation(neg_f[:, :], p_a[0:HG, 0:W], ACT.Copy, scale=-1.0)
                            act.activation(neg_bf[:, n % 2, 0, :], p_a[0:HG, 0:W], ACT.Copy, scale=-1.0).then_inc(neg_read.sem, 1)
                        elif kind == "score":
                            s, p = divmod(n, 2)
                            score_mm.wait(act, it, n + 1)
                            value_mm.wait(act, it, s - 1)
                            act.activation(probs[:, s % 2, 2 * p:2 * p + 2, :], p_s[:, 2 * p:2 * p + 2, 0:W], ACT.Exp,
                                           scale=HD ** -0.5).then_inc(exp_done.sem, 1)
                        elif kind == "raw":
                            value_mm.wait(act, it, (n + 1) * T)
                            attn_done.wait(act, it, n)
                            act.activation(raw[:, :], p_o[:, 0:W], ACT.Copy).then_inc(raw_done.sem, 1)
                        elif kind == "attn":
                            g, blk = unit(n)
                            attn_done.wait(act, it, n + 1)
                            if g == 0:
                                out_mm.wait(act, earlier(it), (blk + 1) * OT // NB)
                            act.activation(a_hi[:, g, blk * W:(blk + 1) * W], attn[:, n % 2, :], ACT.Copy)\
                               .then_inc(a_hi_done.sem, 1)
                        elif kind == "out" and not last_level:
                            out_mm.wait(act, it, n + 1)
                            fine_done.wait(act, it, 0)
                            act.activation(cur[:, n * SEQ:(n + 1) * SEQ, :].rearrange("p s t -> p (s t)"), p_a[:, 0:W], ACT.Identity,
                                           bias=bias_o[:, n:n + 1]).then_inc(out_read.sem, 1)
                        elif kind == "interp":
                            fine_done.wait(act, it, len(RUNS))
                            fine_stored.wait(act, it, 0)
                            act.activation(fine_hi[:, :, :], fine[:, :, :].rearrange("p (c s) t -> p c (s t)", c=2), ACT.Copy)\
                               .then_inc(fine_hi_done.sem, 1)

                act.wait_ge(const_done.sem, 1)
                iterations(act, steps)

            @block.vector
            def _(dve):
                dve.wait_ge(w_in_done.sem, 48)
                dve.wait_ge(w_hi_done.sem, 1)
                dve.tensor_tensor(out=w_lo[:, :], in0=w_stage[:, 0:WCOLS], in1=w_hi[:, :], op=ALU.subtract)\
                   .then_inc(w_lo_done.sem, 1)
                if last_level:
                    dve.tensor_tensor(out=bias_row, in0=consts[:, CBOB:CBOB + E], in1=consts[:, CBUPB:CBUPB + E],
                                      op=ALU.add).then_inc(const_done.sem, 1)
                    xt_biased.open(dve)
                    out_read.open(dve)
                else:
                    dve.tensor_tensor(out=bias_o[:, :], in0=consts[:, CBO:CBO + 2], in1=consts[:, CBUP:CBUP + 2],
                                      op=ALU.add).then_inc(const_done.sem, 1)
                    fine_done.open(dve)
                dve.wait_ge(const_done.sem, 1)

                def steps(tasks, iteration, prev):
                    for kind, k, n in tasks:
                        it = iteration(k)
                        if kind == "max":
                            u, m = divmod(n, MT)
                            max_mm.wait(dve, it, n + 1)
                            if m == 0:
                                neg_mm.wait(dve, it, u - 1)
                            slot = row_max[:, u % 2, :, :].rearrange("p q h -> p (q h)")
                            if KB > 1:
                                out = part_max[:, u % 2, m // KB, m % KB:m % KB + 1]
                            else:
                                out = slot[:, m * QP:(m + 1) * QP]
                            src = p_m[:, m % 2, :].rearrange("p (r t) -> p r t", r=QP) if QP > 1 else p_m[:, m % 2, :]
                            dve.reduce_max(out, src, AX.X).then_inc(max_read.sem, 1)
                            if KB > 1 and m == MT - 1:
                                max_read.wait(dve, it, n + 1)
                                dve.tensor_tensor(out=slot, in0=part_max[:, u % 2, :, 0], in1=part_max[:, u % 2, :, 1], op=ALU.max)\
                                   .then_inc(max_done.sem, 1)
                        elif kind == "v":
                            v_mm.wait(dve, it, n + 1)
                            if last_level:
                                value_mm.wait(dve, earlier(it), STEPS - T + n // SEQ + 1)
                                out = v_aug[:, n, :, 0:HD]
                            else:
                                v_placed.wait(dve, earlier(it), n + 1)
                                out = v_new[:, n, :].rearrange("p (h d) -> p h d", d=HD)
                            dve.tensor_tensor(out=out, in0=p_a[:, 0:E].rearrange("p (h d) -> p h d", d=HD),
                                              in1=consts[:, CBV:CBV + E].rearrange("p (h d) -> p h d", d=HD), op=ALU.add)\
                               .then_inc(v_done.sem, 1)
                        elif kind == "norm":
                            u, part = divmod(n, NP)
                            cols = slice(part * W // NP, (part + 1) * W // NP)
                            if part == 0:
                                raw_done.wait(dve, it, u + 1)
                                a_lo_done.wait(dve, it, u - 1)
                                dve.sem_inc(held.sem, 1)
                            out, inv = attn[:, u % 2, cols], rec[:, part * W // NP // 32:(part + 1) * W // NP // 32]
                            dve.transpose(out, raw[:, cols]).then_inc(turned_done.sem, 1)
                            turned_done.wait(dve, it, n + 1)
                            dve.reciprocal(inv, out.rearrange("p (c r) -> p c r", r=32)[:, :, HD]).then_inc(rec_done.sem, 1)
                            rec_done.wait(dve, it, n + 1)
                            dve.transpose(out, inv.unsqueeze(2).broadcast_to((128, W // NP // 32, 32))).then_inc(spread_done.sem, 1)
                        elif kind == "out" and last_level:
                            xt_loaded[n % 2].wait(dve, it, n // 2 + 1)
                            y_stored[n % 4].wait(dve, it, n // 4)
                            dve.tensor_tensor(out=s_ring[:, n % 4, :], in0=xt_ring[:, n % 2, :], in1=bias_row, op=ALU.add)\
                               .then_inc(xt_biased.sem, 1)
                            out_mm.wait(dve, it, n + 1)
                            xt_biased.wait(dve, it, n + 1)
                            dve.tensor_tensor(out=s_ring[:, n % 4, :], in0=p_a[:, 0:E], in1=s_ring[:, n % 4, :], op=ALU.add)\
                               .then_inc(out_read.sem, 1)
                        elif kind == "stats":
                            out_read.wait(dve, it, n + 1)
                            dve.bn_stats(stats[:, n % 2, :], s_ring[:, n % 4, :]).then_inc(stats_done.sem, 1)
                            stats_done.wait(dve, it, n + 1)
                            dve.sem_inc(held.sem, 1)
                            dve.bn_aggr(moments[:, n % 2, :], stats[:, n % 2, :]).then_inc(moments_done.sem, 1)
                            moments_done.wait(dve, it, n + 1)
                            dve.tensor_scalar(var_eps[:, n % 2:n % 2 + 1], moments[:, n % 2, 1:2], EPS, None, ALU.add)\
                               .then_inc(eps_done.sem, 1)
                        elif kind == "finish":
                            rstd_done.wait(dve, it, n + 1)
                            dve.tensor_scalar(s_ring[:, n % 4, :], s_ring[:, n % 4, :], moments[:, n % 2, 0:1],
                                              rstd[:, n % 2:n % 2 + 1], ALU.subtract, ALU.mult).then_inc(y_done.sem, 1)
                        elif kind == "blend":
                            if n == 0:
                                out_read.wait(dve, it, OT)
                                fine_lo_done.wait(dve, it, 0)
                                dve.tensor_scalar(cur34[:, :, :], cur[:, :, :], 0.75, None, ALU.mult).then_inc(cur34_done.sem, 1)
                                cur34_done.wait(dve, it, 1)
                            src, dst, size, here = RUNS[n]
                            dve.scalar_tensor_tensor(out=fine[:, :, dst:dst + size], in0=cur[:, :, src:src + size],
                                                     scalar=0.25, in1=cur34[:, :, here:here + size],
                                                     op0=ALU.mult, op1=ALU.add).then_inc(fine_done.sem, 1)

                iterations(dve, steps)

            @block.tensor
            def _(pe):
                pe.wait_ge(w_hi_done.sem, 1)
                pe.wait_ge(w_lo_done.sem, 1)
                pe.wait_ge(set_done.sem, 3)
                out_mm.open(pe)

                def three(out, pairs):
                    terms = [t for (a_h, a_l), (b_h, b_l) in pairs for t in ((a_h, b_h), (a_l, b_h), (a_h, b_l))]
                    for n, (a, c) in enumerate(terms):
                        ins = pe.matmul(out, a, c, start=n == 0, stop=n == len(terms) - 1)
                    return ins

                def steps(tasks, iteration, prev):
                    for task in tasks:
                        kind, k, n = task
                        it = iteration(k)
                        if task in prev and prev[task]:
                            was, at, m = prev[task]
                            {"proj": qk_read, "neg": neg_read, "v": v_done, "out": out_read}[was].wait(pe, iteration(at), m + 1)
                        if kind == "proj":
                            t, m, blk = proj(n)
                            if n == 0:
                                x_hi_done.wait(pe, it, 2)
                                x_lo_done.wait(pe, it, 2)
                            cols = [slice(WQK + c * 512 + t * 256 + m * 128, WQK + c * 512 + t * 256 + m * 128 + 128) for c in range(2)]
                            tok = slice(blk * W, (blk + 1) * W)
                            three(p_a[:, 0:W], [((w_hi[:, cols[c]], w_lo[:, cols[c]]), (x_hi[:, c, tok], x_lo[:, c, tok]))
                                                for c in range(2)]).then_inc(qk_mm.sem, 1)
                        elif kind == "neg":
                            if KB > 1:
                                max_done.wait(pe, it, n + 1)
                            else:
                                max_read.wait(pe, it, (n + 1) * MT)
                            for q in range(NQ):
                                ins = pe.transpose(p_a[0:HG, q * 128:(q + 1) * 128], row_max[:, n % 2, q, :], ident[:, :])
                            ins.then_inc(neg_mm.sem, 1)
                        elif kind == "v":
                            at = (n % SEQ) * S + (n // SEQ) * 128
                            tok = slice(at, at + 128)
                            wc = [slice(WV + c * 256, WV + (c + 1) * 256) for c in range(2)]
                            three(p_a[:, 0:E], [((x_hi[:, c, tok], x_lo[:, c, tok]), (w_hi[:, wc[c]], w_lo[:, wc[c]]))
                                                for c in range(2)]).then_inc(v_mm.sem, 1)
                        elif kind == "out":
                            if n == 0:
                                a_lo_done.wait(pe, it, U)
                            if last_level:
                                tok = slice(n * 128, (n + 1) * 128)
                                up_loaded[n % 2].wait(pe, it, n // 2 + 1)
                                pairs = [((a_hi[:, g, tok], a_lo[:, g, tok]),
                                          (w_hi[:, WO + g * E:WO + (g + 1) * E], w_lo[:, WO + g * E:WO + (g + 1) * E])) for g in range(G)]
                                pairs += [((up_ring_hi[:, n % 2, c, :], up_ring_lo[:, n % 2, c, :]),
                                           (w_hi[:, WUP + c * E:WUP + (c + 1) * E], w_lo[:, WUP + c * E:WUP + (c + 1) * E])) for c in range(2)]
                                three(p_a[:, 0:E], pairs).then_inc(out_mm.sem, 1)
                            else:
                                def wcol(base, c):
                                    at = slice(base + c * E + n * 128, base + c * E + n * 128 + 128)
                                    return w_hi[:, at], w_lo[:, at]
                                pairs = [(wcol(WO, g), (a_hi[:, g, :], a_lo[:, g, :])) for g in range(G)]
                                if below:
                                    c_loaded.wait(pe, it, 1)
                                    pairs += [(wcol(WUP, c), (c_hi[:, c, :], c_lo[:, c, :])) for c in range(2)]
                                three(p_a[:, 0:W], pairs).then_inc(out_mm.sem, 1)
                        elif kind == "score":
                            s, p = divmod(n, 2)
                            u, kt = divmod(s, T)
                            g, blk = unit(u)
                            if kt == 0 and p == 0:
                                neg_placed[u % 2].wait(pe, it, u // 2 + 1)
                            exp_done.wait(pe, it, n - 1)
                            for j in (2 * p, 2 * p + 1):
                                for i in range(SEQ):
                                    key, at = i * S + kt * 128, blk * W + i * QS
                                    ins = pe.matmul(p_s[:, j, i * QS:(i + 1) * QS], k_st[0:ROWS + 2, HG * g + j, key:key + 128],
                                                    q_st[0:ROWS + 2, HG * g + j, at:at + QS], start=True, stop=True)
                            ins.then_inc(score_mm.sem, 1)
                        elif kind == "max":
                            u, m = divmod(n, MT)
                            g, blk = unit(u)
                            if m == 0:
                                stacked[g].wait(pe, it, 2 * len(K_PIECES))
                            max_read.wait(pe, it, n - 1)
                            for r in range(QP):
                                head, kb = divmod(m * QP + r, KB)
                                q, j = divmod(head, HG)
                                at = blk * W + q * 128
                                key = at // S * S + kb * QS
                                ins = pe.matmul(p_m[:, m % 2, r * QS:(r + 1) * QS], q_st[0:ROWS, HG * g + j, at:at + 128],
                                                k_st[0:ROWS, HG * g + j, key:key + QS], start=True, stop=True)
                            ins.then_inc(max_mm.sem, 1)
                        elif kind == "value":
                            u, kt = divmod(n, T)
                            g, blk = unit(u)
                            exp_done.wait(pe, it, 2 * n + 2)
                            if u == 0:
                                v_placed.wait(pe, it, (kt + 1) * SEQ)
                            if kt == 0:
                                raw_done.wait(pe, it, u)
                            for i in range(SEQ):
                                cols = slice(i * QS, (i + 1) * QS)
                                for j in range(HG):
                                    ins = pe.matmul(p_o[32 * j:32 * j + 32, cols], v_aug[:, kt * SEQ + i, HG * g + j, :],
                                                    probs[:, n % 2, j, cols], start=kt == 0 and (i == 0 or T == 1),
                                                    stop=kt == T - 1 and (i == SEQ - 1 or T == 1))
                            ins.then_inc(value_mm.sem, 1)

                iterations(pe, steps)

        clear_semaphores(nc, signals)


W1COLS, HCOLS = 512, 1024
USES = 24
W3AT = 8 * W1COLS + 16 * HCOLS
FCOLS = W3AT + 8 * E
TURN = 20


def w_cols(v):
    return (v * W1COLS, W1COLS) if v < 8 else (8 * W1COLS + (v - 8) * HCOLS, HCOLS)


def ffn(nc, x1, wf, scales, s3row, ident_in, lo_scr, out):
    with ExitStack() as ctx:
        def sb(name, shape, dt=F32):
            return ctx.enter_context(nc.sbuf_tensor(f"f_{name}", shape, dt))

        signals = []

        def sig(name, per, step=1, lead=0):
            signals.append(Signal(ctx, nc, f"f_{name}", per, step, lead))
            return signals[-1]

        w_hi = sb("w_hi", [128, FCOLS], F32R)
        w3_lo = sb("w3_lo", [128, 8 * E], F32R)
        lo_ring = sb("lo_ring", [128, 3, HCOLS], F32R)
        xa = sb("xa", [128, 2, 4, E])
        xt_hi, xt_lo = sb("xt_hi", [128, 2, 512], F32R), sb("xt_lo", [128, 2, 512], F32R)
        h_hi, h_lo = sb("h_hi", [128, 2, 8, 512], F32R), sb("h_lo", [128, 2, 8, 512], F32R)
        gate = sb("gate", [128, 2, 512])
        h_f = sb("h_f", [128, 2, 512])
        sc = sb("sc", [128, 32])
        s3 = sb("s3", [128, E])
        ident = sb("ident", [128, 128])
        s_ring = sb("s_ring", [128, 2, E])
        stats, moments = sb("stats", [128, 2, 6]), sb("moments", [128, 2, 2])
        var_eps, rstd, minus_half = sb("var_eps", [128, 2]), sb("rstd", [128, 2]), sb("minus_half", [128, 1])
        lo_max, lo_any, flag = sb("lo_max", [128, USES + 3]), sb("lo_any", [1, 1]), sb("flag", [1, 1], mybir.dt.int32)
        p_h = ctx.enter_context(nc.psum_tensor("p_h", [128, 4, 512], F32))
        p_t = ctx.enter_context(nc.psum_tensor("p_t", [128, 2, 512], F32))
        p_y = ctx.enter_context(nc.psum_tensor("p_y", [128, 2, 512], F32))

        const_in, raw_in = sig("const_in", 0), [sig(f"raw_in{i}", 0) for i in range(4)]
        x_copied = sig("x_copied", 0)
        lo_checked = sig("lo_checked", 0)
        lo_turned = sig("lo_turned", 0)
        prep_hi, prep_lo = sig("prep_hi", 0), sig("prep_lo", 0)
        prep_stored = [sig(f"prep_stored{i}", 0) for i in range(3)]
        set_done = sig("set_done", 0)
        x_in = [sig(f"x_in{i}", 1, 16) for i in range(2)]
        t_mm, t_hi, t_lo = sig("t_mm", 2), sig("t_hi", 2), sig("t_lo", 2)
        lo_in = [sig(f"lo_in{i}", USES // 3, 16) for i in range(3)]
        h_mm = sig("h_mm", 32, lead=3)
        act_read = sig("act_read", 24, lead=4)
        gated = sig("gated", 8, lead=2)
        hi_done, lo_done = sig("hi_done", 24), sig("lo_done", 24, lead=2)
        y_mm, y_scaled, y_sum = sig("y_mm", 4, lead=1), sig("y_scaled", 4, lead=2), sig("y_sum", 4, lead=5)
        stats_done, moments_done = sig("stats_done", 4), sig("moments_done", 4)
        eps_done, rstd_done, y_done = sig("eps_done", 4), sig("rstd_done", 4), sig("y_done", 4)
        stored = [sig(f"stored{i}", 2, 16, lead=1) for i in range(2)]
        held = sig("held", 0)
        PREP = [w_cols(v) for v in range(USES)] + [(W3AT, HCOLS), (W3AT + HCOLS, HCOLS)]

        def bank(v, which=0):
            return 2 * v + which if v < 8 else 16 + v - 8

        def halves(engine, turn, steps):
            turn(0, 0, 0)
            with engine.Fori(0, B) as b:
                for half in range(2):
                    nxt = (lambda b=b, half=half: turn((b, half), 1 - half, (b * 2, half + 1)))
                    steps(b, half, (b * 2, half), nxt)

        def staged(n, k):
            slot = (xa[:, 0, :, :].rearrange("p a e -> p (a e)"), xa[:, 1, :, :].rearrange("p a e -> p (a e)"),
                    gate[:, :, :].rearrange("p a e -> p (a e)"), h_f[:, :, :].rearrange("p a e -> p (a e)"))[n % 4]
            return slot[:, 0:k]

        def lo_of(n, k):
            return w3_lo[:, (n - USES) * HCOLS:(n - USES + 1) * HCOLS] if n >= USES else lo_ring[:, n % 3, 0:k]

        with nc.Block() as block:
            @block.sync
            def _(sp):
                for dst, src in ((sc, scales), (s3, s3row), (ident, ident_in)):
                    sp.dma_start(dst[:, :], src).then_inc(const_in.sem, 16)
                sp.dma_start(x1[B, 0:512, :], x1[0, 0:512, :]).then_inc(x_copied.sem, 16)
                for n in range(len(PREP) + 4):
                    if n >= 4:
                        sp.wait_ge(prep_lo.sem, n - 3)
                        if n - 4 < USES:
                            col, k = PREP[n - 4]
                            sp.dma_start(lo_scr[:, col:col + k], lo_of(n - 4, k).bitcast(F32)).then_inc(prep_stored[(n - 4) % 3].sem, 16)
                    if n < len(PREP):
                        col, k = PREP[n]
                        sp.dma_start(staged(n, k), wf[:, col:col + k]).then_inc(raw_in[n % 4].sem, 16)
                for i in range(3):
                    sp.wait_ge(prep_stored[i].sem, 16 * (USES // 3))
                sp.wait_ge(x_copied.sem, 16)
                sp.wait_ge(lo_checked.sem, len(PREP) + 3)
                has_lo = sp.value_load(flag[0:1, 0:1], min_val=0, max_val=1)

                def turn(b, half, hh):
                    y_sum.wait(sp, hh, -4)
                    sp.sem_inc(held.sem, 1)
                    sp.dma_start(xa[:, half, :, :], x1[number(b), half * 512:(half + 1) * 512, :].rearrange("(q p) e -> p q e", p=128))\
                      .then_inc(x_in[half].sem, 16)

                def steps(b, half, hh, turn_next):
                    with sp.If(has_lo > 0):
                        for v in range(USES):
                            h_mm.wait(sp, hh, (bank(v - 3, 1 if v - 3 < 8 else 0) + 1) if v >= 3 else v - 2)
                            sp.sem_inc(held.sem, 1)
                            col, k = w_cols(v)
                            sp.dma_start(lo_ring[:, v % 3, 0:k].bitcast(F32), lo_scr[:, col:col + k]).then_inc(lo_in[v % 3].sem, 16)
                    turn_next()

                halves(sp, turn, steps)
                x_in[0].wait(sp, B, 1)

            @block.gpsimd
            def _(pool):
                pool.memset(minus_half[:, :], -0.5).then_inc(set_done.sem, 1)
                pool.wait_ge(set_done.sem, 1)
                def turn(b, half, hh):
                    pass

                def steps(b, half, hh, turn_next):
                    for q in range(4):
                        eps_done.wait(pool, hh, q + 1)
                        pool.tensor_tensor(out=rstd[:, q % 2:q % 2 + 1], in0=var_eps[:, q % 2:q % 2 + 1],
                                           in1=minus_half[:, :], op=ALU.pow).then_inc(rstd_done.sem, 1)

                halves(pool, turn, steps)

            @block.scalar
            def _(act):
                for n, (col, k) in enumerate(PREP):
                    act.wait_ge(raw_in[n % 4].sem, 16 * (n // 4 + 1))
                    act.activation(w_hi[:, col:col + k], staged(n, k), ACT.Copy)\
                       .then_inc(prep_hi.sem, 1)
                act.wait_ge(const_in.sem, 48)
                act.sem_inc(act_read.sem, 4)
                for i in range(2):
                    act.sem_inc(stored[i].sem, 16)

                def turn(b, half, hh):
                    h_mm.wait(act, hh, 16 - 32)
                    for c in range(2):
                        t_mm.wait(act, hh, c + 1)
                        act.activation(xt_hi[:, c, :], p_t[:, c, :], ACT.Copy).then_inc(t_hi.sem, 1)

                def steps(b, half, hh, turn_next):
                    for v in range(USES):
                        h_mm.wait(act, hh, bank(v) + 1)
                        if v < 8:
                            gated.wait(act, hh, v - 1)
                            act.activation(gate[:, v % 2, :], p_h[:, bank(v) % 4, :], ACT.Silu, scale=sc[:, v:v + 1])\
                               .then_inc(act_read.sem, 1)
                            gated.wait(act, hh, v + 1)
                        else:
                            lo_done.wait(act, hh, v - 1)
                            act.activation(h_f[:, v % 2, :], p_h[:, bank(v) % 4, :], ACT.Gelu, scale=sc[:, 8 + v:9 + v])\
                               .then_inc(act_read.sem, 1)
                            act_read.wait(act, hh, v + 1)
                        if v == 0:
                            y_mm.wait(act, hh, 0)
                        act.activation(h_hi[:, (v // 8) % 2, v % 8, :], h_f[:, v % 2, :], ACT.Copy).then_inc(hi_done.sem, 1)
                        if v == TURN:
                            turn_next()
                    for q in range(4):
                        y_done.wait(act, hh, q + 1)
                        row = half * 512 + q * 128
                        act.dma_start(out[b, row:row + 128, :], s_ring[:, q % 2, :]).then_inc(stored[q % 2].sem, 16)

                halves(act, turn, steps)
                for i in range(2):
                    act.wait_ge(stored[i].sem, stored[i].at(2 * B - 1, 2))

            @block.vector
            def _(dve):
                for n, (col, k) in enumerate(PREP):
                    dve.wait_ge(prep_hi.sem, n + 1)
                    if 3 <= n < USES:
                        dve.wait_ge(prep_stored[n % 3].sem, 16 * (n // 3))
                        dve.wait_ge(lo_checked.sem, n - 2)
                    dve.tensor_tensor(out=lo_of(n, k), in0=staged(n, k), in1=w_hi[:, col:col + k], op=ALU.subtract)\
                       .then_inc(prep_lo.sem, 1)
                    dve.wait_ge(prep_lo.sem, n + 1)
                    dve.tensor_reduce(lo_max[:, n:n + 1], lo_of(n, k).bitcast(F32), AX.X, ALU.max, apply_absolute_value=True)\
                       .then_inc(lo_checked.sem, 1)
                dve.wait_ge(lo_checked.sem, len(PREP))
                dve.reduce_max(lo_max[:, len(PREP):len(PREP) + 1], lo_max[:, 0:len(PREP)], AX.X).then_inc(lo_checked.sem, 1)
                dve.wait_ge(lo_turned.sem, 1)
                dve.reduce_max(lo_any[0:1, 0:1], p_t[0:1, 0, 0:128], AX.X).then_inc(lo_checked.sem, 1)
                dve.wait_ge(lo_checked.sem, len(PREP) + 2)
                dve.tensor_scalar(flag[0:1, 0:1], lo_any[0:1, 0:1], 0.0, None, ALU.is_gt).then_inc(lo_checked.sem, 1)
                dve.wait_ge(const_in.sem, 48)
                for s, n in ((lo_done, 2), (y_scaled, 2), (y_sum, 5), (gated, 2)):
                    dve.sem_inc(s.sem, n)

                def finish(hh, q):
                    rstd_done.wait(dve, hh, q + 1)
                    dve.tensor_scalar(s_ring[:, q % 2, :], s_ring[:, q % 2, :], moments[:, q % 2, 0:1],
                                      rstd[:, q % 2:q % 2 + 1], ALU.subtract, ALU.mult).then_inc(y_done.sem, 1)

                def turn(b, half, hh):
                    for c in range(2):
                        t_hi.wait(dve, hh, c + 1)
                        dve.tensor_tensor(out=xt_lo[:, c, :], in0=p_t[:, c, :], in1=xt_hi[:, c, :], op=ALU.subtract)\
                           .then_inc(t_lo.sem, 1)

                def steps(b, half, hh, turn_next):
                    for v in range(USES):
                        if v < 8:
                            h_mm.wait(dve, hh, bank(v, 1) + 1)
                            act_read.wait(dve, hh, v + 1)
                            lo_done.wait(dve, hh, v - 1)
                            dve.scalar_tensor_tensor(out=h_f[:, v % 2, :], in0=p_h[:, bank(v, 1) % 4, :], scalar=sc[:, 8 + v:9 + v],
                                                     in1=gate[:, v % 2, :], op0=ALU.mult, op1=ALU.mult).then_inc(gated.sem, 1)
                        hi_done.wait(dve, hh, v + 1)
                        dve.tensor_tensor(out=h_lo[:, (v // 8) % 2, v % 8, :], in0=h_f[:, v % 2, :],
                                          in1=h_hi[:, (v // 8) % 2, v % 8, :], op=ALU.subtract).then_inc(lo_done.sem, 1)
                        if v == TURN:
                            turn_next()
                    for q in range(4):
                        y_mm.wait(dve, hh, q + 1)
                        stored[q % 2].wait(dve, hh, q // 2)
                        dve.tensor_tensor(out=s_ring[:, q % 2, :], in0=p_y[:, q % 2, 0:E], in1=s3[:, :], op=ALU.mult)\
                           .then_inc(y_scaled.sem, 1)
                        y_scaled.wait(dve, hh, q + 1)
                        dve.tensor_tensor(out=s_ring[:, q % 2, :], in0=s_ring[:, q % 2, :], in1=xa[:, half, q, :], op=ALU.add)\
                           .then_inc(y_sum.sem, 1)
                        y_sum.wait(dve, hh, q + 1)
                        dve.bn_stats(stats[:, q % 2, :], s_ring[:, q % 2, :]).then_inc(stats_done.sem, 1)
                        stats_done.wait(dve, hh, q + 1)
                        dve.sem_inc(held.sem, 1)
                        dve.bn_aggr(moments[:, q % 2, :], stats[:, q % 2, :]).then_inc(moments_done.sem, 1)
                        moments_done.wait(dve, hh, q + 1)
                        dve.tensor_scalar(var_eps[:, q % 2:q % 2 + 1], moments[:, q % 2, 1:2], EPS, None, ALU.add)\
                           .then_inc(eps_done.sem, 1)
                        if q > 0:
                            finish(hh, q - 1)
                    finish(hh, 3)

                halves(dve, turn, steps)

            @block.tensor
            def _(pe):
                pe.wait_ge(prep_lo.sem, len(PREP))
                pe.wait_ge(const_in.sem, 48)
                pe.wait_ge(lo_checked.sem, len(PREP) + 1)
                pe.transpose(p_t[0:1, 0, 0:128], lo_max[:, len(PREP):len(PREP) + 1], ident[:, :]).then_inc(lo_turned.sem, 1)
                pe.wait_ge(lo_checked.sem, len(PREP) + 3)
                has_lo = pe.value_load(flag[0:1, 0:1], min_val=0, max_val=1)
                pe.sem_inc(h_mm.sem, 3)
                pe.sem_inc(y_mm.sem, 1)

                def bank_free(hh, u):
                    p = u - 4
                    if 0 <= p < 16 and p % 2:
                        gated.wait(pe, hh, p // 2 + 1)
                    elif 0 <= p < 16:
                        act_read.wait(pe, hh, p // 2 + 1)
                    else:
                        act_read.wait(pe, hh, p + 1 if p < 0 else 8 + p - 16 + 1)

                def turn(b, half, hh):
                    x_in[half].wait(pe, b, 1)
                    t_lo.wait(pe, hh, 0)
                    for c in range(2):
                        for q in range(4):
                            ins = pe.transpose(p_t[:, c, q * 128:(q + 1) * 128], xa[:, half, q, c * 128:(c + 1) * 128], ident[:, :])
                        ins.then_inc(t_mm.sem, 1)

                def split(out, first, last, stationary, moving):
                    terms = [(stationary[0], moving[0]), (stationary[1], moving[0]), (stationary[0], moving[1])]
                    terms = [t for t in terms if t[0] is not None and t[1] is not None]
                    for n, (a, c) in enumerate(terms):
                        ins = pe.matmul(out, a, c, start=first and n == 0, stop=last and n == len(terms) - 1)
                    return ins

                def layers(hh, lo, turn_next):
                    for v in range(USES):
                        if lo:
                            lo_in[v % 3].wait(pe, hh, v // 3 + 1)
                        if v == 0:
                            t_lo.wait(pe, hh, 2)
                        col, _ = w_cols(v)
                        kinds = 2 if v < 8 else 1
                        chunks = 2 if v < 8 else 8
                        for which in range(kinds):
                            u = bank(v, which)
                            bank_free(hh, u)
                            for c in range(chunks):
                                at_c = (which * chunks + c) * 128
                                weights = (w_hi[:, col + at_c:col + at_c + 128], lo_ring[:, v % 3, at_c:at_c + 128] if lo else None)
                                if v < 8:
                                    acts = xt_hi[:, c, :], xt_lo[:, c, :]
                                else:
                                    src = (v // 8 - 1) % 2
                                    if v % 8 == 0:
                                        lo_done.wait(pe, hh, (v // 8 - 1) * 8 + c + 1)
                                    acts = h_hi[:, src, c, :], h_lo[:, src, c, :]
                                ins = split(p_h[:, u % 4, :], c == 0, c == chunks - 1, weights, acts)
                            ins.then_inc(h_mm.sem, 1)
                        if v == TURN:
                            turn_next()
                    for q in range(4):
                        tok = slice(q * 128, (q + 1) * 128)
                        y_scaled.wait(pe, hh, q - 1)
                        for c in range(8):
                            if q == 0:
                                lo_done.wait(pe, hh, 16 + c + 1)
                            at_c = c * E
                            wh, wl = w_hi[:, W3AT + at_c:W3AT + at_c + E], w3_lo[:, at_c:at_c + E] if lo else None
                            ins = split(p_y[:, q % 2, 0:E], c == 0, c == 7, (h_hi[:, 0, c, tok], h_lo[:, 0, c, tok]), (wh, wl))
                        ins.then_inc(y_mm.sem, 1)

                def steps(b, half, hh, turn_next):
                    with pe.If(has_lo > 0):
                        layers(hh, True, turn_next)
                    with pe.Else():
                        layers(hh, False, turn_next)

                halves(pe, turn, steps)


def program(nc, xt, xtok, wpack, cpack, wf, scales, s3row, ident, out):
    scr = nc.dram_tensor("qk_scratch", (2, 3, E, S0), BF16, kind="Internal").ap()
    up_hi = [nc.dram_tensor(f"up_hi{i}", (128, 2, B * (S0 >> i)), F32, kind="Internal").ap() for i in range(LEVELS - 1)]
    up_lo = [nc.dram_tensor(f"up_lo{i}", (128, 2, B * (S0 >> i)), F32, kind="Internal").ap() for i in range(LEVELS - 1)]
    x1 = nc.dram_tensor("x1", (B + 1, S0, E), F32, kind="Internal").ap()
    lo_scr = nc.dram_tensor("w_lo_scratch", (128, FCOLS), F32, kind="Internal").ap()
    for lvl in reversed(range(LEVELS)):
        attention_level(nc, lvl, xt, xtok, wpack, cpack, ident, scr, up_hi, up_lo, x1)
    ffn(nc, x1, wf, scales, s3row, ident, lo_scr, out)


def kernel(**inputs):
    import concourse.bacc as bacc
    from concourse.bass_utils import run_bass_kernel_spmd as run

    a = {k: np.asarray(v) for k, v in inputs.items()}
    f = np.float32
    order = token_order()
    x = a["L0_attn_query"][:, order, :]
    iw, ib = a["L0_attn_in_proj_w"], a["L0_attn_in_proj_b"]

    def chunks(wt):
        return wt.reshape(-1, 128, wt.shape[1]).transpose(1, 0, 2).reshape(128, -1)

    wpack, cpack = np.zeros((LEVELS, 128, WCOLS), f), np.zeros((LEVELS, 128, CCOLS), f)
    for i in range(LEVELS):
        wpack[i, :, WQK:WV] = chunks(iw[i, :2 * E].T)
        wpack[i, :, WV:WO] = chunks(iw[i, 2 * E:].T)
        wo = np.zeros((H, 32, E), f)
        wo[:, :HD] = a["L0_attn_out_w"][i].T.reshape(H, HD, E)
        wpack[i, :, WO:WUP] = chunks(wo.reshape(H * 32, E))
        cpack[i, :, CBQK:CBO] = ib[i, :2 * E].reshape(4, 128).T
        cpack[i, :, CBO:CBUP] = a["L0_attn_out_b"][i].reshape(2, 128).T
        cpack[i, :, CBV:CBOB] = ib[i, 2 * E:]
        cpack[i, :, CBOB:CBUPB] = a["L0_attn_out_b"][i]
        if i < LEVELS - 1:
            wpack[i, :, WUP:] = chunks(a["L0_attn_up_w"][i].T)
            cpack[i, :, CBUP:CBV] = a["L0_attn_up_b"][i].reshape(2, 128).T
            cpack[i, :, CBUPB:] = a["L0_attn_up_b"][i]

    def tiles(*ws):
        return np.concatenate([chunks(w[m * 128:(m + 1) * 128].T) for m in range(8) for w in ws], axis=1)

    wf = np.concatenate([tiles(a["L0_ffn_w1_w"], a["L0_ffn_w2_w"]), tiles(a["L0_ffn_h1_w"]), tiles(a["L0_ffn_h2_w"]),
                         chunks(a["L0_ffn_w3_w"].T)], axis=1)
    scales = np.concatenate([a[f"L0_ffn_{n}_s"].reshape(8, 128).T for n in ("w1", "w2", "h1", "h2")], axis=1)
    arrays = {
        "xt": np.ascontiguousarray(x.transpose(0, 2, 1)), "xtok": np.ascontiguousarray(x), "wpack": wpack, "cpack": cpack,
        "wf": np.ascontiguousarray(wf), "scales": np.ascontiguousarray(scales),
        "s3row": np.ascontiguousarray(np.broadcast_to(a["L0_ffn_w3_s"], (128, E))), "ident": np.eye(128, dtype=f),
    }
    nc = bacc.Bacc("TRN2", target_bir_lowering=False, num_devices=1)
    args = [nc.dram_tensor(k, v.shape, mybir.dt.from_np(v.dtype), kind="ExternalInput").ap() for k, v in arrays.items()]
    args.append(nc.dram_tensor("y", (B, S0, E), F32, kind="ExternalOutput").ap())
    program(nc, *args)
    r = run(nc, [arrays], core_ids=[0])
    return r.results[0]["y"][:, np.argsort(order), :]
```
